# Optimizing a Trainium2 kernel written in Bass

```python
import numpy as np
import jax
import jax.numpy as jnp

def _softmax(x, axis=-1):
    return jax.nn.softmax(x, axis=axis)
def _gelu(x):
    return jax.nn.gelu(x, approximate=True)
def _silu(x):
    return jax.nn.silu(x)
def _sigmoid(x):
    return jax.nn.sigmoid(x)
def _layernorm(x, axis=-1, eps=1e-5):
    m = jnp.mean(x, axis=axis, keepdims=True)
    v = jnp.var(x, axis=axis, keepdims=True)
    return (x - m) / jnp.sqrt(v + eps)
def _scatter_add(tgt, idx, src, axis=0):
    return tgt.at[idx].add(src)
def _segment_sum(src, seg, n):
    return jax.ops.segment_sum(src, seg, n)

kernel_name = 'mk_conv_preact_d2_conv_nchw256_51a3bc'

def setup_inputs(seed: int = 0):
    np.random.seed(seed)
    _w = jnp.asarray
    def _rec_inputs():
        import jax
        import jax.numpy as jnp
        _gk = jax.random.key(seed)
        x = -0.0009896 + 1 * jax.random.normal(jax.random.fold_in(_gk, 1), (8, 256, 28, 28), jnp.float32)
        return x
    x = _rec_inputs()
    def _L0_conv_setup():
        import jax, jax.numpy as jnp
        import numpy as np
        KS = 3
        PAD = 1
        N = KS * KS

        def conv2d(x, w, b=None):
            out = jax.lax.conv_general_dilated(x, w, window_strides=(1, 1), padding=((PAD, PAD), (PAD, PAD)), dimension_numbers=('NCHW', 'OIHW', 'NCHW'))
            if b is not None:
                out = out + b[None, :, None, None]
            return out

        def deform_conv(x, w_p, b_p, w_m, b_m, w_c):
            b, c, h, w = x.shape
            offset = conv2d(x, w_p, b_p)
            m = jax.nn.sigmoid(conv2d(x, w_m, b_m))
            xp = jnp.pad(x, ((0, 0), (0, 0), (PAD, PAD), (PAD, PAD)))
            hp, wp = (h + 2 * PAD, w + 2 * PAD)
            r = jnp.arange(-(KS - 1) // 2, (KS - 1) // 2 + 1, dtype=x.dtype)
            pn_x, pn_y = jnp.meshgrid(r, r, indexing='ij')
            pn = jnp.concatenate([pn_x.reshape(-1), pn_y.reshape(-1)])
            p0_x, p0_y = jnp.meshgrid(jnp.arange(1, h + 1, dtype=x.dtype), jnp.arange(1, w + 1, dtype=x.dtype), indexing='ij')
            p0 = jnp.concatenate([jnp.tile(p0_x[None], (N, 1, 1)), jnp.tile(p0_y[None], (N, 1, 1))])
            p = jnp.transpose(offset + p0[None] + pn[None, :, None, None], (0, 2, 3, 1))
            px, py = (p[..., :N], p[..., N:])
            fx, fy = (jnp.floor(px), jnp.floor(py))
            q_lt_x = jnp.clip(fx, 0, hp - 1)
            q_lt_y = jnp.clip(fy, 0, wp - 1)
            q_rb_x = jnp.clip(fx + 1, 0, hp - 1)
            q_rb_y = jnp.clip(fy + 1, 0, wp - 1)
            px = jnp.clip(px, 0, hp - 1)
            py = jnp.clip(py, 0, wp - 1)
            g_lt = (1 + (q_lt_x - px)) * (1 + (q_lt_y - py))
            g_rb = (1 - (q_rb_x - px)) * (1 - (q_rb_y - py))
            g_lb = (1 + (q_lt_x - px)) * (1 - (q_rb_y - py))
            g_rt = (1 - (q_rb_x - px)) * (1 + (q_lt_y - py))
            xf = xp.reshape(b, c, hp * wp)

            def gather(qx, qy):
                idx = (qx * wp + qy).astype(jnp.int32).reshape(b, 1, h * w * N)
                idx = jnp.broadcast_to(idx, (b, c, h * w * N))
                return jnp.take_along_axis(xf, idx, axis=2).reshape(b, c, h, w, N)
            x_off = g_lt[:, None] * gather(q_lt_x, q_lt_y) + g_rb[:, None] * gather(q_rb_x, q_rb_y) + g_lb[:, None] * gather(q_lt_x, q_rb_y) + g_rt[:, None] * gather(q_rb_x, q_lt_y)
            x_off = x_off * jnp.transpose(m, (0, 2, 3, 1))[:, None]
            return jnp.einsum('bchwn,ocn->bohw', x_off, w_c.reshape(w_c.shape[0], c, N))
        key = jax.random.key(seed)
        ks = jax.random.split(key, 12)
        b, dim, hid, H, W = (8, 256, 1024, 28, 28)
        inp = {'x': jax.random.normal(ks[0], (b, dim, H, W), jnp.float32), 'w_p1': jax.random.normal(ks[1], (2 * N, dim, KS, KS), jnp.float32) * 0.01, 'b_p1': jnp.zeros((2 * N,), jnp.float32), 'w_m1': jax.random.normal(ks[2], (N, dim, KS, KS), jnp.float32) * 0.05, 'b_m1': jnp.zeros((N,), jnp.float32), 'w_c1': jax.random.normal(ks[3], (hid, dim, KS, KS), jnp.float32) * 0.02, 'w_p2': jax.random.normal(ks[4], (2 * N, hid, KS, KS), jnp.float32) * 0.01, 'b_p2': jnp.zeros((2 * N,), jnp.float32), 'w_m2': jax.random.normal(ks[5], (N, hid, KS, KS), jnp.float32) * 0.05, 'b_m2': jnp.zeros((N,), jnp.float32), 'w_c2': jax.random.normal(ks[6], (dim, hid, KS, KS), jnp.float32) * 0.01}
        return inp
    _L0_conv_all = _L0_conv_setup()
    _L0_conv_in = {k: v for k, v in _L0_conv_all.items() if k in ('w_p1', 'b_p1', 'w_m1', 'b_m1', 'w_c1', 'w_p2', 'b_p2', 'w_m2', 'b_m2', 'w_c2', )}
    del _L0_conv_all

    def _L1_conv_setup():
        import jax, jax.numpy as jnp
        import numpy as np
        DIM = 256
        HEADS = 8
        WINDOWS = (1, 2, 4)
        B, H, W = (1, 64, 64)

        def _integral(a):
            s = jnp.cumsum(jnp.cumsum(a, axis=-2), axis=-1)
            pad = [(0, 0)] * (a.ndim - 2) + [(1, 0), (1, 0)]
            return jnp.pad(s, pad)

        def _box(P, ws, Ho, Wo):
            tp = ws - 1
            r = tp // 2
            l = tp - r
            pad = [(0, 0)] * (P.ndim - 2) + [(l, r), (l, r)]
            Pp = jnp.pad(P, pad, mode='edge')
            return Pp[..., ws:ws + Ho, ws:ws + Wo] - Pp[..., ws:ws + Ho, :Wo] - Pp[..., :Ho, ws:ws + Wo] + Pp[..., :Ho, :Wo]
        key = jax.random.key(seed)
        ks = jax.random.split(key, 6)
        x = jax.random.normal(ks[0], (B, DIM, H, W), jnp.float32)
        Wq = jax.random.normal(ks[1], (DIM, DIM), jnp.float32) * 0.05
        Wk = jax.random.normal(ks[2], (DIM, DIM), jnp.float32) * 0.05
        Wv = jax.random.normal(ks[3], (DIM, DIM), jnp.float32) * 0.05
        Wout = jax.random.normal(ks[4], (DIM, DIM * len(WINDOWS)), jnp.float32) * 0.05
        bout = jnp.zeros((DIM,), jnp.float32)
        return {'x': x, 'Wq': Wq, 'Wk': Wk, 'Wv': Wv, 'Wout': Wout, 'bout': bout}
    _L1_conv_all = _L1_conv_setup()
    _L1_conv_in = {k: v for k, v in _L1_conv_all.items() if k in ('Wq', 'Wk', 'Wv', 'Wout', 'bout', )}
    del _L1_conv_all

    return {
        "x": x,
        "L0_conv_w_p1": _L0_conv_in["w_p1"],
        "L0_conv_b_p1": _L0_conv_in["b_p1"],
        "L0_conv_w_m1": _L0_conv_in["w_m1"],
        "L0_conv_b_m1": _L0_conv_in["b_m1"],
        "L0_conv_w_c1": _L0_conv_in["w_c1"],
        "L0_conv_w_p2": _L0_conv_in["w_p2"],
        "L0_conv_b_p2": _L0_conv_in["b_p2"],
        "L0_conv_w_m2": _L0_conv_in["w_m2"],
        "L0_conv_b_m2": _L0_conv_in["b_m2"],
        "L0_conv_w_c2": _L0_conv_in["w_c2"],
        "L1_conv_Wq": _L1_conv_in["Wq"],
        "L1_conv_Wk": _L1_conv_in["Wk"],
        "L1_conv_Wv": _L1_conv_in["Wv"],
        "L1_conv_Wout": _L1_conv_in["Wout"],
        "L1_conv_bout": _L1_conv_in["bout"],
    }

def reference(x, L0_conv_w_p1, L0_conv_b_p1, L0_conv_w_m1, L0_conv_b_m1, L0_conv_w_c1, L0_conv_w_p2, L0_conv_b_p2, L0_conv_w_m2, L0_conv_b_m2, L0_conv_w_c2, L1_conv_Wq, L1_conv_Wk, L1_conv_Wv, L1_conv_Wout, L1_conv_bout):
    import jax
    import jax.numpy as jnp
    def _L0_conv_ref(x, w_p1, b_p1, w_m1, b_m1, w_c1, w_p2, b_p2, w_m2, b_m2, w_c2):
        import jax, jax.numpy as jnp
        import numpy as np
        KS = 3
        PAD = 1
        N = KS * KS

        def conv2d(x, w, b=None):
            out = jax.lax.conv_general_dilated(x, w, window_strides=(1, 1), padding=((PAD, PAD), (PAD, PAD)), dimension_numbers=('NCHW', 'OIHW', 'NCHW'))
            if b is not None:
                out = out + b[None, :, None, None]
            return out

        def deform_conv(x, w_p, b_p, w_m, b_m, w_c):
            b, c, h, w = x.shape
            offset = conv2d(x, w_p, b_p)
            m = jax.nn.sigmoid(conv2d(x, w_m, b_m))
            xp = jnp.pad(x, ((0, 0), (0, 0), (PAD, PAD), (PAD, PAD)))
            hp, wp = (h + 2 * PAD, w + 2 * PAD)
            r = jnp.arange(-(KS - 1) // 2, (KS - 1) // 2 + 1, dtype=x.dtype)
            pn_x, pn_y = jnp.meshgrid(r, r, indexing='ij')
            pn = jnp.concatenate([pn_x.reshape(-1), pn_y.reshape(-1)])
            p0_x, p0_y = jnp.meshgrid(jnp.arange(1, h + 1, dtype=x.dtype), jnp.arange(1, w + 1, dtype=x.dtype), indexing='ij')
            p0 = jnp.concatenate([jnp.tile(p0_x[None], (N, 1, 1)), jnp.tile(p0_y[None], (N, 1, 1))])
            p = jnp.transpose(offset + p0[None] + pn[None, :, None, None], (0, 2, 3, 1))
            px, py = (p[..., :N], p[..., N:])
            fx, fy = (jnp.floor(px), jnp.floor(py))
            q_lt_x = jnp.clip(fx, 0, hp - 1)
            q_lt_y = jnp.clip(fy, 0, wp - 1)
            q_rb_x = jnp.clip(fx + 1, 0, hp - 1)
            q_rb_y = jnp.clip(fy + 1, 0, wp - 1)
            px = jnp.clip(px, 0, hp - 1)
            py = jnp.clip(py, 0, wp - 1)
            g_lt = (1 + (q_lt_x - px)) * (1 + (q_lt_y - py))
            g_rb = (1 - (q_rb_x - px)) * (1 - (q_rb_y - py))
            g_lb = (1 + (q_lt_x - px)) * (1 - (q_rb_y - py))
            g_rt = (1 - (q_rb_x - px)) * (1 + (q_lt_y - py))
            xf = xp.reshape(b, c, hp * wp)

            def gather(qx, qy):
                idx = (qx * wp + qy).astype(jnp.int32).reshape(b, 1, h * w * N)
                idx = jnp.broadcast_to(idx, (b, c, h * w * N))
                return jnp.take_along_axis(xf, idx, axis=2).reshape(b, c, h, w, N)
            x_off = g_lt[:, None] * gather(q_lt_x, q_lt_y) + g_rb[:, None] * gather(q_rb_x, q_rb_y) + g_lb[:, None] * gather(q_lt_x, q_rb_y) + g_rt[:, None] * gather(q_rb_x, q_lt_y)
            x_off = x_off * jnp.transpose(m, (0, 2, 3, 1))[:, None]
            return jnp.einsum('bchwn,ocn->bohw', x_off, w_c.reshape(w_c.shape[0], c, N))
        h = jax.nn.relu(deform_conv(x, w_p1, b_p1, w_m1, b_m1, w_c1))
        return deform_conv(h, w_p2, b_p2, w_m2, b_m2, w_c2)

    def _L1_conv_ref(x, Wq, Wk, Wv, Wout, bout):
        import jax, jax.numpy as jnp
        import numpy as np
        DIM = 256
        HEADS = 8
        WINDOWS = (1, 2, 4)
        B, H, W = (1, 64, 64)

        def _integral(a):
            s = jnp.cumsum(jnp.cumsum(a, axis=-2), axis=-1)
            pad = [(0, 0)] * (a.ndim - 2) + [(1, 0), (1, 0)]
            return jnp.pad(s, pad)

        def _box(P, ws, Ho, Wo):
            tp = ws - 1
            r = tp // 2
            l = tp - r
            pad = [(0, 0)] * (P.ndim - 2) + [(l, r), (l, r)]
            Pp = jnp.pad(P, pad, mode='edge')
            return Pp[..., ws:ws + Ho, ws:ws + Wo] - Pp[..., ws:ws + Ho, :Wo] - Pp[..., :Ho, ws:ws + Wo] + Pp[..., :Ho, :Wo]
        b, C, Hh, Ww = x.shape
        h = HEADS
        d = C // h
        q = jnp.einsum('bchw,oc->bohw', x, Wq).reshape(b * h, d, Hh, Ww)
        k = jnp.einsum('bchw,oc->bohw', x, Wk).reshape(b * h, d, Hh, Ww)
        v = jnp.einsum('bchw,oc->bohw', x, Wv).reshape(b * h, d, Hh, Ww)
        q = jax.nn.sigmoid(q)
        k = jax.nn.sigmoid(k)
        v = v / jnp.maximum(jnp.linalg.norm(v, axis=1, keepdims=True), 1e-12)
        Ik = _integral(k)
        Ikv = _integral(jnp.einsum('bfhw,bghw->bfghw', k, v))
        outs = []
        for w in WINDOWS:
            ws = Hh // w
            wk = _box(Ik, ws, Hh, Ww)
            wkv = _box(Ikv, ws, Hh, Ww)
            attn = jnp.einsum('bdhw,bdfhw->bfhw', q, wkv)
            norm = jnp.einsum('bdhw,bdhw->bhw', q, wk)
            attn = attn / (norm[:, None] + 1e-06)
            outs.append(attn.reshape(b, C, Hh, Ww))
        o = jnp.concatenate(outs, axis=1)
        return jnp.einsum('bchw,oc->bohw', o, Wout) + bout[None, :, None, None]

    def _gn(v, G=32, eps=1e-5):
        B_, C_, H_, W_ = v.shape
        g = v.reshape(B_, G, C_ // G, H_, W_)
        m = jnp.mean(g, axis=(2, 3, 4), keepdims=True)
        s = jnp.var(g, axis=(2, 3, 4), keepdims=True)
        return ((g - m) / jnp.sqrt(s + eps)).reshape(v.shape)

    def _ln_c(v, eps=1e-6):
        m = jnp.mean(v, axis=1, keepdims=True)
        s = jnp.var(v, axis=1, keepdims=True)
        return (v - m) / jnp.sqrt(s + eps)

    def _ln_t(v, eps=1e-5):
        m = jnp.mean(v, axis=-1, keepdims=True)
        s = jnp.var(v, axis=-1, keepdims=True)
        return (v - m) / jnp.sqrt(s + eps)

    def _to_tokens(v):
        B_, C_, H_, W_ = v.shape
        return v.reshape(B_, C_, H_ * W_).transpose(0, 2, 1)
    def _from_tokens(t, like):
        B_, C_, H_, W_ = like.shape
        return t.transpose(0, 2, 1).reshape(B_, C_, H_, W_)

    x = x + _L0_conv_ref(_gn(x), L0_conv_w_p1, L0_conv_b_p1, L0_conv_w_m1, L0_conv_b_m1, L0_conv_w_c1, L0_conv_w_p2, L0_conv_b_p2, L0_conv_w_m2, L0_conv_b_m2, L0_conv_w_c2)
    x = x + _L1_conv_ref(_gn(x), L1_conv_Wq, L1_conv_Wk, L1_conv_Wv, L1_conv_Wout, L1_conv_bout)
    return x


_drawn_inputs = setup_inputs


def setup_inputs(seed=0):
    import zlib

    import numpy as np

    out = dict(_drawn_inputs(seed))
    spreads = {'L0_conv_b_p1': (0.0, 0.35),
     'L0_conv_b_m1': (0.0, 0.8),
     'L0_conv_b_p2': (0.0, 0.53),
     'L0_conv_b_m2': (0.0, 2.0),
     'L1_conv_bout': (0.0, 0.1)}
    factors = {'L1_conv_Wq': 64.0, 'L1_conv_Wk': 64.0}
    for name, (base, spread) in spreads.items():
        noise = np.random.default_rng([zlib.crc32(name.encode()), seed]).standard_normal(out[name].shape)
        drawn = base * np.exp(spread * noise) if base else spread * noise
        out[name] = jnp.asarray(drawn.astype(out[name].dtype))
    for name, factor in factors.items():
        out[name] = (out[name] * factor).astype(out[name].dtype)
    return out
```

```python
from contextlib import ExitStack

import numpy as np

import concourse.bass as bass
from concourse import mybir

ALU = mybir.AluOpType
ACT = mybir.ActivationFunctionType
F32 = mybir.dt.float32
F16 = mybir.dt.float16
I32 = mybir.dt.int32
AX = mybir.AxisListType
ABSMAX = bass.bass_isa.ReduceOp.absmax

B, C, HID, S = 8, 256, 1024, 28
PIX = S * S
TAPS = 9
OFF = 3 * TAPS
RB = 4
BP = RB * S
NB = S // RB
JW = TAPS * BP
CT = C // 128
HT = HID // 128
GROUPS = (tuple(range(0, 4)), tuple(range(4, NB)))
PADW = S + 2
PADN = PADW * PADW
HALF = PIX // 2
FAR = 2.999
GN_EPS = 1e-5
HEADS, HD = 8, 32
WINDOWS = (1, 2, 4)
VW = 2 * HD + 1
Q_UP, S_DOWN, V_UP, O_UP = 2.0 ** 15, 2.0 ** -20, 2.0 ** 8, 2.0 ** 10
NORM_EPS = 1e-6 * Q_UP * Q_UP * S_DOWN * V_UP
W_SLOTS, W_SLOT = 18, 1024
LO_HI = ((0, 0), (1, 0), (0, 1))


def group_of(r):
    return 0 if r in GROUPS[0] else 1


def window_blocks(ws):
    up = (ws - 1) - (ws - 1) // 2
    down = ws - 1 - up
    return -((RB - 1 + down) // RB), (RB - 1 + up) // RB


def constants():
    p = np.arange(128)
    ident = np.eye(128, dtype=np.float32)
    grp = (p[:, None] // 8 == p[None, :] // 8).astype(np.float32) / 8
    sel = ((p[:, None] % 32) == np.arange(OFF)[None]).astype(np.float32)
    n, i, j = np.meshgrid(np.arange(TAPS), np.arange(S), np.arange(S), indexing="ij")
    p0n = np.zeros((OFF, PIX), np.float32)
    p0n[:TAPS] = (i + n // 3 - 1).reshape(TAPS, PIX)
    p0n[TAPS:2 * TAPS] = (j + n % 3 - 1).reshape(TAPS, PIX)
    k = np.arange(OFF)
    rows = np.stack([k < 2 * TAPS, k >= 2 * TAPS, k < TAPS], 1).astype(np.float32)
    q = np.arange(BP)
    negq = np.stack([-(RB * t + q // S) for t in range(NB)] + [-(q % S)], 1).astype(np.float32)
    masks = np.zeros((BP, len(WINDOWS), 2 * NB - 1, RB, S), np.float16)
    for w, div in enumerate(WINDOWS):
        ws = S // div
        up = (ws - 1) - (ws - 1) // 2
        down = ws - 1 - up
        for d in range(2 * NB - 1):
            row = (RB * (d - NB + 1) + np.arange(RB))[None] - (q // S)[:, None]
            col = np.arange(S)[None] - (q % S)[:, None]
            ok = lambda x: (x >= -down) & (x <= up)
            masks[:, w, d] = ok(row)[:, :, None] & ok(col)[:, None, :]
    return {"ident": ident, "grp": grp, "sel": sel, "p0n": p0n, "rows": rows, "negq": negq,
            "masks": masks.reshape(BP, len(WINDOWS), -1)}


START = 1


def since(count):
    return count + START


def power_of_two(dve, sem, most, scale, inverse):
    def as_int(t):
        return t.bitcast(I32)
    dve.tensor_scalar(most, most, 1e-30, None, ALU.max).then_inc(sem, 1)
    dve.wait_ge(sem, since(1))
    dve.tensor_scalar(as_int(scale), as_int(most), 0x7F800000, None, ALU.bitwise_and).then_inc(sem, 1)
    dve.wait_ge(sem, since(2))
    dve.tensor_scalar(as_int(inverse), as_int(scale), -1.0, float(0x7F000000), ALU.mult, ALU.add
                      ).then_inc(sem, 1)
    dve.wait_ge(sem, since(3))


def three_passes(pe, out, lhs, rhs, start, stop):
    for i, (a, b) in enumerate(LO_HI):
        mm = pe.matmul(out, lhs(a), rhs(b), start=start and i == 0, stop=stop and i == 2,
                       skip_group_check=True)
    return mm



GN_STEPS = B * CT * 3


def gn_buffers(sb):
    class Gn:
        stats = sb("stats", [128, B * CT, 2, 6])
        agg = sb("agg", [128, B * CT, 2])
        means, dev, var = (sb(n, [128, B * CT]) for n in ("means", "dev", "var"))
        cols = sb("cols", [128, B, 2 * CT])
    return Gn


def gn_statistics_dve(dve, s_img, img, gn, k):
    n = 0
    for b in range(B):
        dve.wait_ge(s_img[b], since(16))
        for ct in range(CT):
            for h in range(2):
                dve.bn_stats(gn.stats[:, b * CT + ct, h, :],
                             img(ct, b)[:, h * HALF:(h + 1) * HALF]).then_inc(k.s_gn, 1)
                n += 1
    dve.wait_ge(k.s_gn, since(n))
    for i in range(B * CT):
        dve.bn_aggr(gn.agg[:, i, :], gn.stats[:, i, :, :]).then_inc(k.s_gn, 1)
        n += 1
    dve.wait_ge(k.s_gn, since(n))
    dve.tensor_copy(gn.means[:], gn.agg[:, :, 0]).then_inc(k.s_gn, 1)
    dve.wait_ge(k.s_gmm, since(1))
    by_image = gn.cols[:, :, 0:CT]
    dve.tensor_copy(by_image, gn.ps_mean.rearrange("p (b c) -> p b c", c=CT)).then_inc(k.s_gn, 1)
    dve.wait_ge(k.s_gn, since(n + 2))
    dev = gn.dev[:].rearrange("p (b c) -> p b c", c=CT)
    dve.tensor_tensor(dev, gn.means[:].rearrange("p (b c) -> p b c", c=CT), by_image, ALU.subtract
                      ).then_inc(k.s_gn, 1)
    dve.wait_ge(k.s_gn, since(n + 3))
    dve.tensor_tensor(gn.dev[:], gn.dev[:], gn.dev[:], ALU.mult).then_inc(k.s_gn, 1)
    dve.wait_ge(k.s_gn, since(n + 4))
    dve.tensor_tensor(gn.var[:], gn.agg[:, :, 1], gn.dev[:], ALU.add).then_inc(k.s_gn, 1)
    dve.wait_ge(k.s_gmm, since(2))
    dve.tensor_scalar(gn.var[:], gn.ps_var, GN_EPS, None, ALU.add).then_inc(k.s_gn, 1)
    dve.wait_ge(k.s_sqrt, since(1))
    dve.reciprocal(gn.cols[:, :, CT:2 * CT], dev).then_inc(k.s_gn, 1)
    dve.wait_ge(k.s_gn, since(n + 7))


def gn_statistics_pe(pe, grp, gn, k):
    pe.wait_ge(k.s_gn, since(GN_STEPS + 1))
    pe.matmul(gn.ps_mean, grp[:], gn.means[:], start=True, stop=True).then_inc(k.s_gmm, 1)
    pe.wait_ge(k.s_gn, since(GN_STEPS + 5))
    pe.matmul(gn.ps_var, grp[:], gn.var[:], start=True, stop=True).then_inc(k.s_gmm, 1)


def gn_statistics_act(act, gn, k):
    act.wait_ge(k.s_gn, since(GN_STEPS + 6))
    act.activation(gn.dev[:], gn.var[:], ACT.Sqrt).then_inc(k.s_sqrt, 1)



def offset_conv_pe(pe, ps, w, xp, tiles):
    steps = [(kt, n, a, b) for kt in range(tiles) for n in range(TAPS) for a, b in LO_HI]
    for half in range(2):
        for i, (kt, n, a, b) in enumerate(steps):
            g = i % 4
            top = n // 3 + half * (S // 2)
            mm = pe.matmul(ps[32 * g:32 * g + 32, half, 0:HALF], w(kt, n, a),
                           xp(kt, b)[:, top:top + S // 2, n % 3:n % 3 + S], start=i < 4,
                           stop=i >= len(steps) - 4, skip_group_check=True)
    return mm


def offsets_act(act, b, psA, psB, quarters, scale, bias, offs, msk, k):
    act.wait_ge(k.s_conv, since(b + 1))
    act.wait_ge(k.s_sum, since(2 * b))
    for h in range(2):
        act.activation(quarters[:, h, :], psA[:, h, 0:HALF], ACT.Copy).then_inc(k.s_quarters, 1)
    act.wait_ge(k.s_pos, since(2 * b))
    act.wait_ge(k.s_reach, since(b))
    for h in range(2):
        act.wait_ge(k.s_sum, since(2 * b + h + 1))
        act.activation(offs[:, h, :], psB[0:OFF, h, 0:HALF], ACT.Identity, bias=bias[:, 0:1],
                       scale=scale).then_inc(k.s_offs, 1)
    act.wait_ge(k.s_posout, since(32 * b))
    for h in range(2):
        act.activation(msk[:, h, :], psB[0:OFF, h, 0:HALF], ACT.Sigmoid, bias=bias[:, 0:1],
                       scale=scale).then_inc(k.s_msk, 1)


def positions_dve(dve, b, offs, p0n, pos, reach, k):
    dve.wait_ge(k.s_posout, since(32 * b))
    for h in range(2):
        dve.wait_ge(k.s_offs, since(2 * b + h + 1))
        dve.tensor_tensor(pos[:, h, :], offs[:, h, :], p0n[:, h * HALF:(h + 1) * HALF],
                          ALU.add).then_inc(k.s_pos, 1)
    dve.tensor_reduce(reach[0:OFF, bass.ds(b, 1)], offs[:], AX.XY, ALU.max,
                      apply_absolute_value=True).then_inc(k.s_reach, 1)


def sum_quarters_pe(pe, b, psB, sel, quarters, k):
    pe.wait_ge(k.s_offs, since(2 * b))
    pe.wait_ge(k.s_msk, since(2 * b))
    for h in range(2):
        pe.wait_ge(k.s_quarters, since(2 * b + h + 1))
        pe.matmul(psB[0:OFF, h, 0:HALF], sel[:], quarters[:, h, :], start=True, stop=True
                  ).then_inc(k.s_sum, 1)


def store_positions_sp(sp, b, to, pos, msk, k):
    sp.wait_ge(k.s_pos, since(2 * (b + 1)))
    sp.wait_ge(k.s_msk, since(2 * (b + 1)))
    to = to.rearrange("r (k q) -> k r q", q=BP)
    view = lambda t: t[:].rearrange("k h q -> k (h q)").rearrange("k (r q) -> k r q", q=BP)
    sp.dma_start(to[0:2 * TAPS], view(pos)[0:2 * TAPS]).then_inc(k.s_posout, 16)
    sp.dma_start(to[2 * TAPS:OFF], view(msk)[2 * TAPS:OFF]).then_inc(k.s_posout, 16)


def far_flag_dve(dve, reach, rows, flag, k):
    dve.wait_ge(k.s_reach, since(B))
    dve.tensor_reduce(reach[:, B:B + 1], reach[:, 0:B], AX.X, ALU.max).then_inc(k.s_far, 1)
    dve.wait_ge(k.s_far, since(1))
    dve.tensor_scalar(reach[0:OFF, B:B + 1], reach[0:OFF, B:B + 1], rows[:, 2:3], None, ALU.mult
                      ).then_inc(k.s_far, 1)
    dve.wait_ge(k.s_far, since(3))
    dve.tensor_scalar(flag, reach[:, B + 1:B + 2], FAR, None, ALU.is_gt).then_inc(k.s_far, 1)


def far_flag_pool(pool, reach, k):
    pool.wait_ge(k.s_far, since(2))
    pool.partition_all_reduce(reach[:, B + 1:B + 2], reach[:, B:B + 1], 128, ABSMAX
                              ).then_inc(k.s_far, 1)


def semaphore(nc, name):
    s = nc.alloc_semaphore(name)
    nc.gpsimd.sem_inc(s, START)
    return s


def stage_block(nc, c):
    nc.all_engine_barrier()
    return c.enter_context(nc.Block())


def semaphores(nc, stage, names):
    return [semaphore(nc, f"{stage}_{n}") for n in names.split()]


SCALES = {"w1": 0, "p1": 1, "m1": 2, "w2": 3, "p2": 4, "m2": 5, "h": 6, "q": 7, "k": 8, "v": 9, "o": 10}


class Kept:

    def __init__(self, nc, ctx):
        def sb(name, shape, dt=F32):
            return ctx.enter_context(nc.sbuf_tensor(name, shape, dt))
        self.ident = sb("ident_s", [128, 128])
        self.grp = sb("grp_s", [128, 128])
        self.sel = sb("sel_s", [128, OFF])
        self.negq = sb("negq_s", [BP, NB + 1])
        self.rows = sb("rows_s", [OFF, 3])
        self.scale = sb("scale_w", [128, len(SCALES)])
        self.inv = sb("inv_w", [128, len(SCALES)])
        self.hmax = sb("hmax", [128, 2])
        self.far = sb("far", [128, 2], I32)

    def scale_of(self, name, parts=128):
        return self.scale[0:parts, SCALES[name]:SCALES[name] + 1]

    def inv_of(self, name, parts=128):
        return self.inv[0:parts, SCALES[name]:SCALES[name] + 1]


class Weights:

    def __init__(self, nc, ctx):
        self.big = ctx.enter_context(nc.sbuf_tensor("weights", [128, W_SLOTS + 1, 2 * W_SLOT], F16))

    def words(self, c):
        return self.big[:, c, :].bitcast(F32)

    def half(self, c, h):
        return self.big[:, c, h * W_SLOT:(h + 1) * W_SLOT]

    def load(self, sp, src, k):
        for c in range(W_SLOTS):
            sp.dma_start(self.words(c + 1), src[:, c * W_SLOT:(c + 1) * W_SLOT]).then_inc(k.s_w, 16)

    def largest(self, dve, maxes, k):
        dve.wait_ge(k.s_w, since(16 * W_SLOTS))
        for c in range(W_SLOTS):
            dve.tensor_reduce(maxes[:, c:c + 1], self.words(c + 1), AX.X, ALU.max,
                              apply_absolute_value=True).then_inc(k.s_wmax, 1)
        dve.wait_ge(k.s_wmax, since(W_SLOTS))
        dve.tensor_reduce(maxes[:, W_SLOTS:W_SLOTS + 1], maxes[:, 0:W_SLOTS], AX.X, ALU.max
                          ).then_inc(k.s_wmax, 1)

    def split_high(self, act, inv, k):
        act.wait_ge(k.s_wscale, since(3))
        for c in range(W_SLOTS):
            if c:
                act.wait_ge(k.s_wlo, since(c))
            act.activation(self.half(c, 0), self.words(c + 1), ACT.Copy, scale=inv
                           ).then_inc(k.s_whi, 1)

    def split_low(self, dve, inv, k):
        for c in range(W_SLOTS):
            dve.wait_ge(k.s_whi, since(c + 1))
            dve.scalar_tensor_tensor(self.half(c, 1), self.words(c + 1), inv, self.half(c, 0),
                                     ALU.mult, ALU.subtract).then_inc(k.s_wlo, 1)


def largest_weight_pool(pool, maxes, most, k):
    pool.wait_ge(k.s_wmax, since(W_SLOTS + 1))
    pool.partition_all_reduce(most[:], maxes[:, W_SLOTS:W_SLOTS + 1], 128, ABSMAX
                              ).then_inc(k.s_wmax, 1)


def offset_weights_dve(dve, wo32, wo, maxes2, most2, osc, kept, k, p, m, extra=None):
    dve.wait_ge(k.s_wo, since(16))
    for i, (a, z) in enumerate(((0, 2 * TAPS), (2 * TAPS, OFF))):
        dve.tensor_reduce(maxes2[:, i:i + 1], wo32[:, :, a:z], AX.XY, ALU.max,
                          apply_absolute_value=True).then_inc(k.s_womax, 1)
    dve.wait_ge(k.s_womax, since(3))
    i = SCALES[p]
    power_of_two(dve, k.s_woscale, most2[:], kept.scale[:, i:i + 2], kept.inv[:, i:i + 2])
    dve.tensor_scalar(osc[:, 0:1], kept.rows[:, 0:1], kept.scale_of(p, OFF), None, ALU.mult
                      ).then_inc(k.s_osc, 1)
    dve.wait_ge(k.s_osc, since(1))
    dve.scalar_tensor_tensor(osc[:, 1:2], kept.rows[:, 1:2], kept.scale_of(m, OFF), osc[:, 0:1],
                             ALU.mult, ALU.add).then_inc(k.s_osc, 1)
    dve.wait_ge(k.s_osc, since(2))
    if extra is not None:
        dve.tensor_scalar(osc[:, 1:2], osc[:, 1:2], extra, None, ALU.mult).then_inc(k.s_osc, 1)
    dve.wait_ge(k.s_wohi, since(2))
    for a, z, name in ((0, 2 * TAPS, p), (2 * TAPS, OFF, m)):
        dve.scalar_tensor_tensor(wo[:, 1, :, a:z], wo32[:, :, a:z], kept.inv_of(name),
                                 wo[:, 0, :, a:z], ALU.mult, ALU.subtract).then_inc(k.s_wolo, 1)


def offset_weights_pool(pool, maxes2, most2, k):
    pool.wait_ge(k.s_womax, since(2))
    pool.partition_all_reduce(most2[:], maxes2[:], 128, ABSMAX).then_inc(k.s_womax, 1)


def offset_weights_act(act, wo32, wo, kept, k, p, m):
    act.wait_ge(k.s_zero, since(1))
    act.wait_ge(k.s_woscale, since(3))
    for a, z, name in ((0, 2 * TAPS, p), (2 * TAPS, OFF, m)):
        act.activation(wo[:, 0, :, a:z], wo32[:, :, a:z], ACT.Copy, scale=kept.inv_of(name)
                       ).then_inc(k.s_wohi, 1)



TWOS = [slice(t, min(t + 2, NB)) for t in range(0, NB, 2)]


def two(ps, i, ts):
    return ps[:, i, 0:(ts.stop - ts.start) * C].rearrange("p (t c) -> p t c", c=C)


def stage_norm(nc, kept, wts, x, w1, woff1, boff1, consts, xT_d, pos_d):
    with ExitStack() as c:
        def sb(name, shape, dt=F32):
            return c.enter_context(nc.sbuf_tensor("n_" + name, shape, dt))

        def psum(name, shape, dt=F32):
            return c.enter_context(nc.psum_tensor("n_" + name, shape, dt))

        xs = sb("x", [128, CT, B, PIX])
        xn = sb("xn", [128, CT, PIX])
        xp = sb("xp", [128, CT, 2, PADW, PADW], F16)
        xt = sb("xt", [BP, NB, 2, C], F16)
        gn = gn_buffers(sb)
        cur = sb("cur", [128, 2 * CT])
        wo32 = sb("wo32", [128, CT * TAPS, OFF])
        wo = sb("wo", [128, 2, CT * TAPS, 32], F16)
        maxes, most = sb("maxes", [128, W_SLOTS + 1]), sb("most", [128, 1])
        maxes2, most2 = sb("maxes2", [128, 2]), sb("most2", [128, 2])
        bo, osc = sb("bo", [OFF, 1]), sb("osc", [OFF, 2])
        p0n = sb("p0n", [OFF, PIX])
        quarters = sb("quarters", [128, 2, HALF])
        offs, pos, msk = (sb(n, [OFF, 2, HALF]) for n in ("offs", "pos", "msk"))
        reach = sb("reach", [128, B + 2])
        psA, psB = psum("psA", [128, 2, 512]), psum("psB", [128, 2, 512])
        psT = psum("psT", [BP, 4, 512])
        class Sem:
            (s_const, s_wo, s_w, s_gn, s_gmm, s_sqrt, s_womax, s_woscale, s_wohi, s_wolo, s_osc,
             s_wmax, s_wscale, s_whi, s_wlo, s_zero, s_cur, s_xn, s_xphi, s_xplo, s_tr, s_xthi,
             s_xtlo, s_xtout, s_conv, s_quarters, s_sum, s_pos, s_msk, s_offs, s_reach, s_posout,
             s_far) = semaphores(
                nc, "n",
                "const wo w gn gmm sqrt womax woscale wohi wolo osc wmax wscale whi wlo zero cur "
                "xn xphi xplo tr xthi xtlo xtout conv quarters sum pos msk offs reach posout far")
        k = Sem
        s_img = [semaphore(nc, f"n_x{b}") for b in range(B)]
        gn.ps_mean, gn.ps_var = psA[:, 0, 0:B * CT], psA[:, 1, 0:B * CT]
        block = stage_block(nc, c)

        @block.sync
        def _(sp):
            for t, name in ((kept.grp, "grp"), (kept.ident, "ident"), (kept.sel, "sel"),
                            (kept.negq, "negq"), (kept.rows, "rows"), (p0n, "p0n")):
                sp.dma_start(t[:], consts[name]).then_inc(k.s_const, 16)
            sp.dma_start(bo[:], boff1).then_inc(k.s_const, 16)
            sp.dma_start(wo32[:], woff1).then_inc(k.s_wo, 16)
            for b in range(B):
                sp.dma_start(xs[:, :, b, :], x[b].rearrange("(k p) i j -> p k (i j)", p=128)
                             ).then_inc(s_img[b], 16)
            wts.load(sp, w1, k)
            with sp.Fori(0, B) as b:
                sp.wait_ge(k.s_xthi, since(len(TWOS) * (b + 1)))
                sp.wait_ge(k.s_xtlo, since(len(TWOS) * (b + 1)))
                sp.dma_start(xT_d[b], xt[:].rearrange("p t h c -> p (t h c)")).then_inc(k.s_xtout, 16)
                store_positions_sp(sp, b, pos_d[b], pos, msk, k)
            sp.wait_ge(k.s_xtout, since(16 * B))
            sp.wait_ge(k.s_posout, since(32 * B))

        @block.gpsimd
        def _(pool):
            pool.memset(wo[:], 0.0).then_inc(k.s_zero, 1)
            pool.memset(xp[:], 0.0).then_inc(k.s_zero, 1)
            pool.memset(reach[:], 0.0).then_inc(k.s_zero, 1)
            offset_weights_pool(pool, maxes2, most2, k)
            far_flag_pool(pool, reach, k)
            largest_weight_pool(pool, maxes, most, k)

        @block.vector
        def _(dve):
            dve.wait_ge(k.s_const, since(16 * 7))
            offset_weights_dve(dve, wo32, wo, maxes2, most2, osc, kept, k, "p1", "m1")
            gn_statistics_dve(dve, s_img, lambda ct, b: xs[:, ct, b, :], gn, k)
            dve.wait_ge(k.s_zero, since(3))
            with dve.Fori(0, B) as b:
                dve.tensor_copy(cur[:], gn.cols[:, bass.ds(b, 1), :].rearrange("p b c -> p (b c)")
                                ).then_inc(k.s_cur, 1)
                dve.wait_ge(k.s_cur, since(b + 1))
                dve.wait_ge(k.s_tr, since(len(TWOS) * b))
                dve.wait_ge(k.s_xphi, since(CT * b))
                for ct in range(CT):
                    img = xs[:, ct, bass.ds(b, 1), :].rearrange("p b q -> p (b q)")
                    dve.tensor_scalar(xn[:, ct, :], img, cur[:, ct:ct + 1],
                                      cur[:, CT + ct:CT + ct + 1], ALU.subtract, ALU.mult
                                      ).then_inc(k.s_xn, 1)
                for ct in range(CT):
                    dve.wait_ge(k.s_xphi, since(CT * b + ct + 1))
                    dve.tensor_tensor(xp[:, ct, 1, 1:1 + S, 1:1 + S],
                                      xn[:, ct, :].rearrange("p (i j) -> p i j", j=S),
                                      xp[:, ct, 0, 1:1 + S, 1:1 + S], ALU.subtract
                                      ).then_inc(k.s_xplo, 1)
                for i, ts in enumerate(TWOS):
                    dve.wait_ge(k.s_xthi, since(len(TWOS) * b + i + 1))
                    dve.tensor_tensor(xt[:, ts, 1, :], two(psT, i, ts), xt[:, ts, 0, :],
                                      ALU.subtract).then_inc(k.s_xtlo, 1)
                positions_dve(dve, b, offs, p0n, pos, reach, k)
            far_flag_dve(dve, reach, kept.rows, kept.far[:, 0:1], k)
            wts.largest(dve, maxes, k)
            dve.wait_ge(k.s_wmax, since(W_SLOTS + 2))
            power_of_two(dve, k.s_wscale, most[:], kept.scale_of("w1"), kept.inv_of("w1"))
            wts.split_low(dve, kept.inv_of("w1"), k)

        @block.scalar
        def _(act):
            offset_weights_act(act, wo32, wo, kept, k, "p1", "m1")
            gn_statistics_act(act, gn, k)
            act.wait_ge(k.s_zero, since(3))
            act.wait_ge(k.s_const, since(16 * 7))
            act.wait_ge(k.s_osc, since(2))
            with act.Fori(0, B) as b:
                act.wait_ge(k.s_conv, since(b))
                for ct in range(CT):
                    act.wait_ge(k.s_xn, since(CT * b + ct + 1))
                    act.activation(xp[:, ct, 0, 1:1 + S, 1:1 + S],
                                   xn[:, ct, :].rearrange("p (i j) -> p i j", j=S), ACT.Copy
                                   ).then_inc(k.s_xphi, 1)
                act.wait_ge(k.s_xtout, since(16 * b))
                for i, ts in enumerate(TWOS):
                    act.wait_ge(k.s_tr, since(len(TWOS) * b + i + 1))
                    act.activation(xt[:, ts, 0, :], two(psT, i, ts), ACT.Copy).then_inc(k.s_xthi, 1)
                offsets_act(act, b, psA, psB, quarters, osc[:, 1:2], bo, offs, msk, k)
            wts.split_high(act, kept.inv_of("w1"), k)

        @block.tensor
        def _(pe):
            pe.wait_ge(k.s_const, since(16 * 7))
            gn_statistics_pe(pe, kept.grp, gn, k)
            pe.wait_ge(k.s_wolo, since(2))
            with pe.Fori(0, B) as b:
                pe.wait_ge(k.s_xn, since(CT * (b + 1)))
                pe.wait_ge(k.s_xtlo, since(len(TWOS) * b))
                for t in range(NB):
                    for ct in range(CT):
                        mm = pe.transpose(psT[:, t // 2, (t % 2) * C + ct * 128:
                                              (t % 2) * C + (ct + 1) * 128],
                                          xn[:, ct, t * BP:(t + 1) * BP], kept.ident[:])
                    if t % 2 or t == NB - 1:
                        mm.then_inc(k.s_tr, 1)
                pe.wait_ge(k.s_xplo, since(CT * (b + 1)))
                pe.wait_ge(k.s_quarters, since(2 * b))
                offset_conv_pe(pe, psA, lambda kt, n, h: wo[:, h, kt * TAPS + n, :],
                               lambda kt, h: xp[:, kt, h], CT).then_inc(k.s_conv, 1)
                sum_quarters_pe(pe, b, psB, kept.sel, quarters, k)



class Plan:

    def __init__(self, pairs, kept_blocks):
        self.pairs, self.loads, self.load_of = pairs, [], []
        for u, t, r in pairs:
            if r not in self.loads[-kept_blocks:]:
                self.loads.append(r)
            self.load_of.append(max(m for m, x in enumerate(self.loads) if x == r))
        loads = range(len(self.loads))
        self.first = [self.load_of.index(m) for m in loads]
        self.last = [max(n for n, x in enumerate(self.load_of) if x == m) for m in loads]

    def of_unit(self, u):
        return [n for n, p in enumerate(self.pairs) if p[0] == u]


def earlier(b, n, slots, per_image):
    return per_image * b + max(0, n - slots + 1)


def wait_both(sp, first, second):
    for _, count in (first, second):
        if not isinstance(count, int):
            sp.to_reg(since(count))
    sp.wait_ge(first[0], since(first[1]))
    sp.wait_ge(second[0], since(second[1]))


class Sampler:

    def __init__(self, nc, c, stage, kept, plan, pos_slots, g_at, g_free):
        def sb(name, shape, dt=F32):
            return c.enter_context(nc.sbuf_tensor(f"{stage}_{name}", shape, dt))
        self.kept, self.plan, self.slots = kept, plan, pos_slots
        self.row = sb("row", [BP, pos_slots, JW])
        self.cm = sb("cm", [BP, 2, 2, JW])
        self.dcol = sb("dcol", [BP, JW])
        self.col = sb("col", [BP, pos_slots, JW])
        self.drow = sb("drow", [BP, 2, JW])
        self.g = sb("g", [BP, 3, JW])
        self.g_at, self.g_free = g_at, g_free
        class Sem:
            (s_dcol, s_hcol, s_col, s_drow, s_g, s_ghi, s_glo) = semaphores(
                nc, stage,
                "dcol hcol col drow g ghi glo")
        self.k = Sem
        self.s_rowin = [semaphore(nc, f"{stage}_rowin{i}") for i in range(pos_slots)]
        self.s_cmin = [semaphore(nc, f"{stage}_cmin{i}") for i in range(2)]
        self.acts, self.dves = 0, 0

    def load(self, sp, b, n, pos_d):
        k, p = self.k, self.plan
        L, P, slot = len(p.loads), len(p.pairs), n % self.slots
        rows_used = P * b + (p.last[n - self.slots] + 1 if n >= self.slots else 0)
        wait_both(sp, (k.s_col, earlier(b, n, 2, L)), (k.s_drow, rows_used))
        src = pos_d[b, p.loads[n]]
        sp.dma_start(self.cm[:, n % 2].rearrange("p k j -> p (k j)"),
                     src[JW:3 * JW].partition_broadcast(BP)).then_inc(self.s_cmin[n % 2], 16)
        sp.dma_start(self.row[:, slot, :], src[0:JW].partition_broadcast(BP)
                     ).then_inc(self.s_rowin[slot], 16)

    def landed(self, eng, sems, b, m):
        L, slots = len(self.plan.loads), len(sems)
        in_slot = len(range(m % slots, L, slots))
        eng.wait_ge(sems[m % slots], since(16 * (in_slot * b + m // slots + 1)))

    def act(self, act, b, upto):
        k, p, negq = self.k, self.plan, self.kept.negq
        L, P = len(p.loads), len(p.pairs)
        start, upto = self.acts, min(upto, P)
        for n in range(start, upto):
            t, m = p.pairs[n][1], p.load_of[n]
            if p.first[m] == n:
                self.landed(act, self.s_cmin, b, m)
                act.wait_ge(k.s_col, since(L * b + m))
                act.activation(self.dcol[:], self.cm[:, m % 2, 0, :], ACT.Abs,
                               bias=negq[:, NB:NB + 1]).then_inc(k.s_dcol, 1)
                self.landed(act, self.s_rowin, b, m)
            act.wait_ge(k.s_g, since(P * b + max(0, n - 1)))
            act.activation(self.drow[:, n % 2, :], self.row[:, m % self.slots, :], ACT.Abs,
                           bias=negq[:, t:t + 1]).then_inc(k.s_drow, 1)
            if n > start:
                self.clamp(act, b, n - 1)
        if upto > start:
            self.clamp(act, b, upto - 1)
            self.acts = upto

    def clamp(self, act, b, n):
        k, P = self.k, len(self.plan.pairs)
        self.g_free(act, b, n)
        act.wait_ge(k.s_g, since(P * b + n + 1))
        out, shape = self.g_at(n, 0)
        act.activation(out, shape(self.g[:, n % 3, :]), ACT.Relu).then_inc(k.s_ghi, 1)

    def dve(self, dve, b, upto):
        k, p = self.k, self.plan
        L, P = len(p.loads), len(p.pairs)
        start, upto = self.dves, min(upto, P)
        for n in range(start, upto):
            t, m = p.pairs[n][1], p.load_of[n]
            if p.first[m] == n:
                dve.wait_ge(k.s_dcol, since(L * b + m + 1))
                dve.tensor_scalar(self.dcol[:], self.dcol[:], 1.0, 1.0, ALU.min, ALU.subtract
                                  ).then_inc(k.s_hcol, 1)
                dve.wait_ge(k.s_hcol, since(L * b + m + 1))
                dve.tensor_tensor(self.col[:, m % self.slots, :], self.dcol[:],
                                  self.cm[:, m % 2, 1, :], ALU.mult).then_inc(k.s_col, 1)
            dve.wait_ge(k.s_drow, since(P * b + n + 1))
            dve.wait_ge(k.s_col, since(L * b + m + 1))
            dve.wait_ge(k.s_glo, since(P * b + max(0, n - 2)))
            dve.scalar_tensor_tensor(self.g[:, n % 3, :], self.drow[:, n % 2, :], 1.0,
                                     self.col[:, m % self.slots, :], ALU.subtract, ALU.mult
                                     ).then_inc(k.s_g, 1)
            if n > start:
                self.low(dve, b, n - 1)
        if upto > start:
            self.low(dve, b, upto - 1)
            self.dves = upto

    def low(self, dve, b, n):
        k, P = self.k, len(self.plan.pairs)
        dve.wait_ge(k.s_ghi, since(P * b + n + 1))
        (hi, shape), (lo, _) = self.g_at(n, 0), self.g_at(n, 1)
        dve.scalar_tensor_tensor(lo, shape(self.g[:, n % 3, :]), 0.0, hi, ALU.max, ALU.subtract
                                 ).then_inc(k.s_glo, 1)


def neighbours(r, band):
    return [x for x in range(NB) if abs(x - r) <= band]


NEAR, ANY = 1, NB


def both_bands(eng, kept, flag, emit):
    far = eng.value_load(kept.far[0:1, flag:flag + 1], min_val=0, max_val=1)
    with eng.If(far < 1):
        emit(NEAR)
    with eng.If(far > 0):
        emit(ANY)



def stage_layer1(nc, kept, wts, xT_d, pos_d, h_d):
    with ExitStack() as c:
        def sb(name, shape, dt=F32):
            return c.enter_context(nc.sbuf_tensor("l_" + name, shape, dt))

        def psum(name, shape, dt=F32):
            return c.enter_context(nc.psum_tensor("l_" + name, shape, dt))

        GS = 4
        xt = sb("xt", [BP, NB, 2, C], F16)
        g = sb("gh", [BP, GS, 2, JW], F16)
        xo = sb("xo", [128, CT, 2, RB, JW], F16)
        hb = sb("h", [128, RB, HT, BP])
        peak = sb("peak", [128, 2])
        ps_x = psum("ps_x", [128, 2 * CT, 512])
        ps_h = psum("ps_h", [128, 4, 512])
        class Sem:
            (s_xtin, s_pair, s_xo, s_xohi, s_xolo, s_conv, s_h, s_hout, s_peak, s_hmax, s_zero) = semaphores(
                nc, "l",
                "xtin pair xo xohi xolo conv h hout peak hmax zero")
        k = Sem
        g_at = lambda n, h: (g[:, n % GS, h, :], lambda v: v)
        plans = {band: Plan([(r, t, r) for r in range(NB) for t in neighbours(r, band)], 1)
                 for band in (NEAR, ANY)}
        smp = Sampler(nc, c, "l", kept, None, 2, g_at, None)
        smp.g_free = lambda act, b, n: act.wait_ge(k.s_pair, since(earlier(b, n, GS, len(smp.plan.pairs))))
        block = stage_block(nc, c)

        def start(band):
            smp.plan, smp.acts, smp.dves = plans[band], 0, 0

        def half(h):
            return slice(h * (JW // 2), (h + 1) * (JW // 2))

        def sample_block(pe, b, plan, r):
            pairs = plan.of_unit(r)
            for n in pairs:
                pe.wait_ge(smp.k.s_glo, since(len(plan.pairs) * b + n + 1))
                t = plan.pairs[n][1]
                for ct in range(CT):
                    for h in range(2):
                        if n == pairs[0]:
                            pe.wait_ge(k.s_xolo, since(4 * NB * b + max(0, 4 * (r - 1) + 2 * ct + h + 1)))
                        mm = three_passes(pe, ps_x[:, 2 * ct + h, 0:JW // 2],
                                          lambda a: xt[:, t, a, ct * 128:(ct + 1) * 128],
                                          lambda a: g[:, n % GS, a, half(h)],
                                          n == pairs[0], n == pairs[-1])
                        if n == pairs[-1] and 2 * ct + h < 3:
                            mm.then_inc(k.s_xo, 1)
                mm.then_inc(k.s_pair, 1)

        @block.sync
        def _(sp):
            def store_h(b, i):
                sp.wait_ge(k.s_h, since(HT * (2 * b + i + 1)))
                for j, r in enumerate(GROUPS[i]):
                    sp.dma_start(h_d[b, r], hb[:, j].rearrange("p m q -> p (m q)")
                                 ).then_inc(k.s_hout, 16)

            def image(b, first):
                for r in range(NB):
                    if r == 2:
                        if not first:
                            store_h(b - 1, 1)
                        sp.wait_ge(k.s_pair, since(len(smp.plan.pairs) * b))
                        sp.dma_start(xt[:].rearrange("p t h c -> p (t h c)"), xT_d[b]
                                     ).then_inc(k.s_xtin, 16)
                    if r == GROUPS[1][0] + 1:
                        store_h(b, 0)
                    smp.load(sp, b, r, pos_d)

            def emit(band):
                start(band)
                image(0, True)
                with sp.Fori(1, B) as b:
                    image(b, False)
                store_h(B - 1, 1)
                sp.wait_ge(k.s_hout, since(16 * NB * B))
            both_bands(sp, kept, 0, emit)

        @block.scalar
        def _(act):
            def emit(band):
                start(band)
                plan = smp.plan
                with act.Fori(0, B) as b:
                    for i, rs in enumerate(GROUPS):
                        for j, r in enumerate(rs):
                            smp.act(act, b, plan.last[r] + 1)
                            smp.act(act, b, plan.last[r] + GS)
                            act.wait_ge(k.s_conv, since(HT * (2 * b + i)))
                            for ct in range(CT):
                                for h in range(2):
                                    q = 2 * ct + h
                                    if q < 3:
                                        act.wait_ge(k.s_xo, since(3 * (NB * b + r) + q + 1))
                                    else:
                                        act.wait_ge(k.s_pair, since(len(plan.pairs) * b + plan.last[r] + 1))
                                    act.activation(xo[:, ct, 0, j, half(h)],
                                                   ps_x[:, 2 * ct + h, 0:JW // 2], ACT.Copy
                                                   ).then_inc(k.s_xohi, 1)
                        act.wait_ge(k.s_hout, since(16 * (NB * b + (RB if i else 0))))
                        act.wait_ge(k.s_peak, since(2 * b + i))
                        for m in range(HT):
                            act.wait_ge(k.s_conv, since(HT * (2 * b + i) + m + 1))
                            act.activation(hb[:, 0:len(rs), m, :],
                                           ps_h[:, m % 4, 0:len(rs) * BP]
                                           .rearrange("p (r q) -> p r q", q=BP), ACT.Relu,
                                           scale=kept.scale_of("w1")).then_inc(k.s_h, 1)
                    smp.acts = 0
            both_bands(act, kept, 0, emit)

        @block.vector
        def _(dve):
            dve.memset(kept.hmax[:], 0.0).then_inc(k.s_zero, 1)
            dve.wait_ge(k.s_zero, since(1))

            def emit(band):
                start(band)
                plan = smp.plan
                with dve.Fori(0, B) as b:
                    for i, rs in enumerate(GROUPS):
                        for j, r in enumerate(rs):
                            smp.dve(dve, b, plan.last[r] + 1)
                            smp.dve(dve, b, plan.last[r] + GS)
                            for ct in range(CT):
                                for h in range(2):
                                    q = 4 * (NB * b + r) + 2 * ct + h
                                    dve.wait_ge(k.s_xohi, since(q + 1))
                                    dve.tensor_tensor(xo[:, ct, 1, j, half(h)],
                                                      ps_x[:, 2 * ct + h, 0:JW // 2],
                                                      xo[:, ct, 0, j, half(h)], ALU.subtract
                                                      ).then_inc(k.s_xolo, 1)
                        dve.wait_ge(k.s_h, since(HT * (2 * b + i + 1)))
                        dve.tensor_reduce(peak[:, 0:1], hb[:, 0:len(rs)], AX.XYZ, ALU.max
                                          ).then_inc(k.s_peak, 1)
                        dve.wait_ge(k.s_peak, since(2 * b + i + 1))
                        dve.tensor_tensor(kept.hmax[:, 0:1], kept.hmax[:, 0:1], peak[:, 0:1],
                                          ALU.max).then_inc(k.s_hmax, 1)
                        dve.wait_ge(k.s_hmax, since(2 * b + i + 1))
                    smp.dves = 0
            both_bands(dve, kept, 0, emit)

        @block.tensor
        def _(pe):
            def emit(band):
                start(band)
                plan = smp.plan
                with pe.Fori(0, B) as b:
                    pe.wait_ge(k.s_xtin, since(16 * (b + 1)))
                    for i, rs in enumerate(GROUPS):
                        for r in rs:
                            sample_block(pe, b, plan, r)
                        pe.wait_ge(k.s_xolo, since(4 * (NB * b + rs[-1] + 1)))
                        for m in range(HT):
                            pe.wait_ge(k.s_h, since(earlier(2 * b + i, m, 4, HT)))
                            for kt in range(CT * TAPS):
                                ct, n = divmod(kt, TAPS)
                                mm = three_passes(
                                    pe, ps_h[:, m % 4, 0:len(rs) * BP],
                                    lambda a: wts.half(kt, a)[:, m * 128:(m + 1) * 128],
                                    lambda a: xo[:, ct, a, 0:len(rs), n * BP:(n + 1) * BP],
                                    kt == 0, kt == CT * TAPS - 1)
                            mm.then_inc(k.s_conv, 1)
            both_bands(pe, kept, 0, emit)



def stage_offsets2(nc, kept, wts, w2, woff2, boff2, consts, h_d, pos_d):
    with ExitStack() as c:
        def sb(name, shape, dt=F32):
            return c.enter_context(nc.sbuf_tensor("o_" + name, shape, dt))

        def psum(name, shape, dt=F32):
            return c.enter_context(nc.psum_tensor("o_" + name, shape, dt))

        HS = 3
        hs = sb("h", [128, HS, HT, BP])
        hp = sb("hp", [128, 2, HT, 2, PADW, PADW], F16)
        wo32 = sb("wo32", [128, HT * TAPS, OFF])
        wo = sb("wo", [128, 2, HT * TAPS, 32], F16)
        maxes, most = sb("maxes", [128, W_SLOTS + 1]), sb("most", [128, 1])
        maxes2, most2 = sb("maxes2", [128, 2]), sb("most2", [128, 2])
        bo, osc = sb("bo", [OFF, 1]), sb("osc", [OFF, 2])
        p0n = sb("p0n", [OFF, PIX])
        quarters = sb("quarters", [128, 2, HALF])
        offs, pos, msk = (sb(n, [OFF, 2, HALF]) for n in ("offs", "pos", "msk"))
        reach = sb("reach", [128, B + 2])
        psA, psB = psum("psA", [128, 2, 512]), psum("psB", [128, 2, 512])
        class Sem:
            (s_const, s_wo, s_w, s_womax, s_woscale, s_wohi, s_wolo, s_osc, s_wmax, s_wscale, s_whi,
             s_wlo, s_hall, s_hscale, s_zero, s_hs, s_hphi, s_hplo, s_conv, s_quarters, s_sum,
             s_pos, s_msk, s_offs, s_reach, s_posout, s_far) = semaphores(
                nc, "o",
                "const wo w womax woscale wohi wolo osc wmax wscale whi wlo hall hscale zero hs "
                "hphi hplo conv quarters sum pos msk offs reach posout far")
        k = Sem
        s_hin = [semaphore(nc, f"o_hin{i}") for i in range(HS)]
        block = stage_block(nc, c)
        ROUND = 2 * NB
        USES = [len(range(i, ROUND, HS)) for i in range(HS)]

        def by_image(eng, first, second):
            first(0, 0)
            first(0, 1)
            second(0)
            with eng.Fori(1, B // 2) as bb:
                first(bb, 0)
                second(2 * bb - 1)
                first(bb, 1)
                second(2 * bb)
            second(B - 1)

        def inner(half, i, t):
            return hp[:, i, :, half, 1 + RB * t:1 + RB * (t + 1), 1:1 + S]

        def as_rows(slot):
            return hs[:, slot].rearrange("p m (i j) -> p m i j", j=S)

        @block.sync
        def _(sp):
            sp.dma_start(p0n[:], consts["p0n"]).then_inc(k.s_const, 16)
            sp.dma_start(bo[:], boff2).then_inc(k.s_const, 16)
            sp.dma_start(wo32[:], woff2).then_inc(k.s_wo, 16)

            def load(bb, i):
                for n in range(NB * i, NB * (i + 1)):
                    sp.wait_ge(k.s_hplo, since(earlier(bb, n, HS, ROUND)))
                    sp.dma_start(hs[:, n % HS].rearrange("p m q -> p (m q)"),
                                 h_d[bb * 2 + i, n % NB]).then_inc(s_hin[n % HS], 16)
            by_image(sp, load, lambda b: store_positions_sp(sp, b, pos_d[b], pos, msk, k))
            wts.load(sp, w2, k)
            sp.wait_ge(k.s_posout, since(32 * B))

        @block.gpsimd
        def _(pool):
            pool.memset(wo[:], 0.0).then_inc(k.s_zero, 1)
            pool.partition_all_reduce(kept.hmax[:, 1:2], kept.hmax[:, 0:1], 128, ABSMAX
                                      ).then_inc(k.s_hall, 1)
            pool.memset(hp[:], 0.0).then_inc(k.s_zero, 1)
            pool.memset(reach[:], 0.0).then_inc(k.s_zero, 1)
            offset_weights_pool(pool, maxes2, most2, k)
            far_flag_pool(pool, reach, k)
            largest_weight_pool(pool, maxes, most, k)

        @block.vector
        def _(dve):
            dve.wait_ge(k.s_hall, since(1))
            power_of_two(dve, k.s_hscale, kept.hmax[:, 1:2], kept.scale_of("h"), kept.inv_of("h"))
            dve.wait_ge(k.s_const, since(16 * 2))
            offset_weights_dve(dve, wo32, wo, maxes2, most2, osc, kept, k, "p2", "m2",
                               kept.scale_of("h", OFF))
            dve.wait_ge(k.s_zero, since(3))

            def split(bb, i):
                for t in range(NB):
                    n = NB * i + t
                    dve.wait_ge(s_hin[n % HS], since(16 * (USES[n % HS] * bb + n // HS + 1)))
                    dve.tensor_scalar(hs[:, n % HS], hs[:, n % HS], kept.inv_of("h"), None,
                                      ALU.mult).then_inc(k.s_hs, 1)
                    dve.wait_ge(k.s_hphi, since(ROUND * bb + n + 1))
                    for m in range(HT):
                        ins = dve.tensor_tensor(inner(1, i, t)[:, m], as_rows(n % HS)[:, m],
                                                inner(0, i, t)[:, m], ALU.subtract)
                    ins.then_inc(k.s_hplo, 1)
            by_image(dve, split, lambda b: positions_dve(dve, b, offs, p0n, pos, reach, k))
            far_flag_dve(dve, reach, kept.rows, kept.far[:, 1:2], k)
            wts.largest(dve, maxes, k)
            dve.wait_ge(k.s_wmax, since(W_SLOTS + 2))
            power_of_two(dve, k.s_wscale, most[:], kept.scale_of("w2"), kept.inv_of("w2"))
            wts.split_low(dve, kept.inv_of("w2"), k)

        @block.scalar
        def _(act):
            offset_weights_act(act, wo32, wo, kept, k, "p2", "m2")
            act.wait_ge(k.s_zero, since(3))
            act.wait_ge(k.s_const, since(16 * 2))
            act.wait_ge(k.s_osc, since(3))

            def split(bb, i):
                if not (isinstance(bb, int) and bb == 0):
                    act.wait_ge(k.s_conv, since(2 * bb + i - 1))
                for t in range(NB):
                    n = NB * i + t
                    act.wait_ge(k.s_hs, since(ROUND * bb + n + 1))
                    for m in range(HT):
                        ins = act.activation(inner(0, i, t)[:, m], as_rows(n % HS)[:, m], ACT.Copy)
                    ins.then_inc(k.s_hphi, 1)
            by_image(act, split, lambda b: offsets_act(act, b, psA, psB, quarters, osc[:, 1:2], bo,
                                                       offs, msk, k))
            wts.split_high(act, kept.inv_of("w2"), k)

        @block.tensor
        def _(pe):
            pe.wait_ge(k.s_wolo, since(2))
            with pe.Fori(0, B // 2) as bb:
                for i in range(2):
                    b = 2 * bb + i
                    pe.wait_ge(k.s_hplo, since(NB * (b + 1)))
                    pe.wait_ge(k.s_quarters, since(2 * b))
                    offset_conv_pe(pe, psA, lambda kt, n, h: wo[:, h, kt * TAPS + n, :],
                                   lambda kt, h: hp[:, i, kt, h], HT).then_inc(k.s_conv, 1)
                    sum_quarters_pe(pe, b, psB, kept.sel, quarters, k)



def stage_layer2(nc, kept, wts, h_d, pos_d, x, x1_d):
    with ExitStack() as c:
        def sb(name, shape, dt=F32):
            return c.enter_context(nc.sbuf_tensor("m_" + name, shape, dt))

        def psum(name, shape, dt=F32):
            return c.enter_context(nc.psum_tensor("m_" + name, shape, dt))

        WIDE = 3 * BP
        YC = [(2 * j, min(2, TAPS - 2 * j)) for j in range(5)]
        NY = len(YC)
        YS = 4
        hs = sb("h", [128, 2, HT * BP])
        hh = sb("hh", [128, 2, 2, HT, BP], F16)
        g = sb("gh", [BP, 2, 2, TAPS, WIDE], F16)
        ys = sb("y", [BP, YS, 2, 2 * C], F16)
        xr = sb("xr", [128, CT, PIX])
        sw = sb("sw", [128, 1])
        ps_y = psum("ps_y", [BP, YS, 512])
        ps_o = psum("ps_o", [128, 2 * CT, 512])
        class Sem:
            (s_hs, s_hhhi, s_hhlo, s_y, s_yhi, s_ylo, s_unit, s_out, s_fin, s_xin, s_xout, s_sw) = semaphores(
                nc, "m",
                "hs hhhi hhlo y yhi ylo unit out fin xin xout sw")
        k = Sem
        s_hin = [semaphore(nc, f"m_hin{i}") for i in range(2)]

        def units(band):
            if band == NEAR:
                return [(t, neighbours(t, NEAR)) for t in range(NB)]
            return [(t, list(range(a, min(a + 3, NB)))) for t in range(NB) for a in range(0, NB, 3)]

        UN = {band: units(band) for band in (NEAR, ANY)}
        plans = {band: Plan([(u, t, r) for u, (t, rs) in enumerate(UN[band]) for r in rs],
                            3 if band == NEAR else 1) for band in (NEAR, ANY)}
        now = {}

        def g_at(n, h):
            u, _, r = smp.plan.pairs[n]
            at = (r - now["units"][u][1][0]) * BP
            return g[:, u % 2, h, :, at:at + BP], lambda v: v.rearrange("p (k q) -> p k q", q=BP)

        def g_free(act, b, n):
            u = smp.plan.pairs[n][0]
            act.wait_ge(k.s_unit, since(earlier(b, u, 2, len(now["units"]))))

        smp = Sampler(nc, c, "m", kept, None, 4, g_at, g_free)
        block = stage_block(nc, c)

        def start(band):
            smp.plan, smp.acts, smp.dves = plans[band], 0, 0
            now["units"] = UN[band]

        def pieces(u):
            rs = now["units"][u][1]
            for i, grp in enumerate(GROUPS):
                both = [r for r in rs if r in grp]
                if both:
                    a, w = (both[0] - rs[0]) * BP, len(both) * BP
                    at = (both[0] - grp[0]) * BP
                    yield i, slice(a, a + w), slice(at, at + w)

        @block.sync
        def _(sp):
            def store(b):
                sp.wait_ge(k.s_fin, since(2 * CT * (b + 1)))
                sp.dma_start(x1_d[b], xr[:].rearrange("p k q -> p (k q)")).then_inc(k.s_xout, 16)

            def emit(band):
                start(band)
                U = len(now["units"])

                def image(b, first):
                    done = 0
                    for u in range(U):
                        sp.wait_ge(k.s_hhlo, since(earlier(b, u, 2, U)))
                        sp.dma_start(hs[:, u % 2], h_d[b, now["units"][u][0]]
                                     ).then_inc(s_hin[u % 2], 16)
                        need = smp.plan.load_of[smp.plan.of_unit(u)[-1]] + 1
                        for m in range(done, need):
                            smp.load(sp, b, m, pos_d)
                        done = need
                        if u == 2:
                            if not first:
                                store(b - 1)
                            sp.wait_ge(k.s_xout, since(16 * b))
                            sp.dma_start(xr[:], x[b].rearrange("(k p) i j -> p k (i j)", p=128)
                                         ).then_inc(k.s_xin, 16)

                image(0, True)
                with sp.Fori(1, B) as b:
                    image(b, False)
                store(B - 1)
                sp.wait_ge(k.s_xout, since(16 * B))
            both_bands(sp, kept, 1, emit)

        def hin(eng, b, u, U):
            eng.wait_ge(s_hin[u % 2], since(16 * (len(range(u % 2, U, 2)) * b + u // 2 + 1)))

        def used(eng, b, y, U):
            n = y - YS
            if n < 0:
                eng.wait_ge(k.s_unit, since(U * b))
            elif n % NY == NY - 1:
                eng.wait_ge(k.s_unit, since(U * b + n // NY + 1))
            else:
                eng.wait_ge(k.s_out, since((NY - 1) * (U * b + n // NY) + n % NY + 1))

        @block.scalar
        def _(act):
            def emit(band):
                start(band)
                U = len(now["units"])

                def split(b, u):
                    hin(act, b, u, U)
                    act.wait_ge(k.s_y, since(NY * earlier(b, u, 2, U)))
                    act.activation(hh[:, u % 2, 0].rearrange("p m q -> p (m q)"), hs[:, u % 2],
                                   ACT.Copy, scale=kept.inv_of("h")).then_inc(k.s_hhhi, 1)

                with act.Fori(0, B) as b:
                    split(b, 0)
                    smp.act(act, b, smp.plan.of_unit(0)[-1] + 1)
                    for u in range(U):
                        ahead = smp.plan.of_unit(u + 1) if u + 1 < U else []
                        for j, (n0, nt) in enumerate(YC):
                            y = NY * u + j
                            act.wait_ge(k.s_y, since(NY * U * b + y + 1))
                            used(act, b, y, U)
                            act.activation(ys[:, y % YS, 0, 0:nt * C], ps_y[:, y % YS, 0:nt * C],
                                           ACT.Copy).then_inc(k.s_yhi, 1)
                            if ahead and j == 1:
                                split(b, u + 1)
                            if ahead and 1 <= j <= len(ahead):
                                smp.act(act, b, ahead[j - 1] + 1)
                    smp.acts = 0
            both_bands(act, kept, 1, emit)

        @block.vector
        def _(dve):
            dve.tensor_tensor(sw[:], kept.scale_of("w2"), kept.scale_of("h"), ALU.mult
                              ).then_inc(k.s_sw, 1)
            dve.wait_ge(k.s_sw, since(1))

            def emit(band):
                start(band)
                U = len(now["units"])

                def split(b, u):
                    dve.wait_ge(k.s_hhhi, since(U * b + u + 1))
                    dve.scalar_tensor_tensor(hh[:, u % 2, 1].rearrange("p m q -> p (m q)"),
                                             hs[:, u % 2], kept.inv_of("h"),
                                             hh[:, u % 2, 0].rearrange("p m q -> p (m q)"),
                                             ALU.mult, ALU.subtract).then_inc(k.s_hhlo, 1)

                with dve.Fori(0, B) as b:
                    split(b, 0)
                    smp.dve(dve, b, smp.plan.of_unit(0)[-1] + 1)
                    for u in range(U):
                        ahead = smp.plan.of_unit(u + 1) if u + 1 < U else []
                        for j, (n0, nt) in enumerate(YC):
                            y = NY * u + j
                            dve.wait_ge(k.s_yhi, since(NY * U * b + y + 1))
                            dve.tensor_tensor(ys[:, y % YS, 1, 0:nt * C], ps_y[:, y % YS, 0:nt * C],
                                              ys[:, y % YS, 0, 0:nt * C], ALU.subtract
                                              ).then_inc(k.s_ylo, 1)
                            if ahead and j == 1:
                                split(b, u + 1)
                            if ahead and 1 <= j <= len(ahead):
                                smp.dve(dve, b, ahead[j - 1] + 1)
                    smp.dves = 0
                    dve.wait_ge(k.s_unit, since(U * (b + 1)))
                    dve.wait_ge(k.s_xin, since(16 * (b + 1)))
                    for mt in range(CT):
                        for i, grp in enumerate(GROUPS):
                            w = len(grp) * BP
                            into = xr[:, mt, grp[0] * BP:grp[0] * BP + w]
                            dve.scalar_tensor_tensor(into, ps_o[:, 2 * mt + i, 0:w], sw[:, 0:1],
                                                     into, ALU.mult, ALU.add).then_inc(k.s_fin, 1)
            both_bands(dve, kept, 1, emit)

        @block.tensor
        def _(pe):
            def emit(band):
                start(band)
                U = len(now["units"])

                def products(b, u, j):
                    n0, nt = YC[j]
                    y = NY * u + j
                    if j == 0:
                        pe.wait_ge(k.s_hhlo, since(U * b + u + 1))
                    pe.wait_ge(k.s_ylo, since(earlier(b, y, YS, NY * U)))
                    for m in range(HT):
                        at = 4096 * j + m * nt * C
                        mm = three_passes(pe, ps_y[:, y % YS, 0:nt * C],
                                          lambda a: hh[:, u % 2, a, m, :],
                                          lambda a: wts.half(at // W_SLOT, a)
                                          [:, at % W_SLOT:at % W_SLOT + nt * C],
                                          m == 0, m == HT - 1)
                    mm.then_inc(k.s_y, 1)

                def sample(b, u, j, begun):
                    n0, nt = YC[j]
                    y = NY * u + j
                    if j == 0:
                        pe.wait_ge(smp.k.s_glo, since(len(smp.plan.pairs) * b
                                   + smp.plan.of_unit(u)[-1] + 1))
                    if u == 0 and j == 0:
                        pe.wait_ge(k.s_fin, since(2 * CT * b))
                    pe.wait_ge(k.s_ylo, since(NY * U * b + y + 1))
                    for d in range(nt):
                        for mt in range(CT):
                            for i, cols, at in pieces(u):
                                first = (mt, i) not in begun
                                begun.add((mt, i))
                                mm = three_passes(
                                    pe, ps_o[:, 2 * mt + i, at],
                                    lambda a: ys[:, y % YS, a, d * C + mt * 128:
                                                 d * C + (mt + 1) * 128],
                                    lambda a: g[:, u % 2, a, n0 + d, cols], first, True)
                    mm.then_inc(k.s_unit if j == NY - 1 else k.s_out, 1)

                with pe.Fori(0, B) as b:
                    begun = set()
                    steps = [(u, j) for u in range(U) for j in range(NY)]
                    products(b, 0, 0)
                    for n, (u, j) in enumerate(steps):
                        if n + 1 < len(steps):
                            products(b, *steps[n + 1])
                        sample(b, u, j, begun)
            both_bands(pe, kept, 1, emit)



def stage_attention(nc, kept, ins, x1_d, qk_d, out):
    with ExitStack() as c:
        def sb(name, shape, dt=F32):
            return c.enter_context(nc.sbuf_tensor("a_" + name, shape, dt))

        def psum(name, shape, dt=F32):
            return c.enter_context(nc.psum_tensor("a_" + name, shape, dt))

        NW, KT = len(WINDOWS), len(WINDOWS) * CT
        CW = NW * VW
        reaches = [window_blocks(S // w) for w in WINDOWS]

        def reached(w, t):
            return [r for r in range(NB) if reaches[w][0] <= r - t <= reaches[w][1]]

        wide = [max(len(reached(w, t)) for t in range(NB)) * BP for w in range(NW)]
        xb = sb("x", [128, 2, CT, PIX])
        xn = sb("xn", [128, CT, PIX])
        xh = sb("xh", [128, CT, 2, PIX], F16)
        gn = gn_buffers(sb)
        cur = sb("cur", [128, 2 * CT])
        wqkv = sb("wqkv", [128, 2, CT, 3, C], F16)
        wo = sb("wo", [128, 2, KT, C], F16)
        maxes, most = sb("maxes", [128, 4]), sb("most", [128, 4])
        so = sb("so", [128, 1])
        bo = sb("bo", [128, CT])
        qf = sb("qf", [128, 2, PIX])
        qh = sb("qh", [128, 2 * CT, 2, PIX], F16)
        stacks = sb("stacks", [96, 2, HEADS, PIX], F16)
        vf = sb("vf", [BP, NB, C])
        norm = sb("norm", [BP, 2, NB * HEADS])
        v = sb("v", [BP, NB, HEADS, VW], F16)
        sh = sb("sh", [BP, 2, 2, PIX], F16)
        sm = [sb(f"sm{w}", [BP, 2, 2, wide[w]], F16) for w in range(NW)]
        masks = sb("masks", [BP, NW, (2 * NB - 1) * BP], F16)
        av = sb("av", [BP, NB * NW, VW])
        rec = sb("rec", [BP, 2, NB * NW])
        num = sb("num", [BP, NB * NW, HD])
        o = sb("o", [128, NB * NW, C])
        ot = sb("ot", [128, KT, 2, PIX], F16)
        sq = ot[0:BP].rearrange("p k h q -> p (k h q)").bitcast(F32)[:, 0:NB * C]
        w32 = o[:].rearrange("p a b -> p (a b)")
        w32qkv = w32[:, 0:CT * 3 * C].rearrange("p (t i o) -> p t i o", t=CT, i=3)
        w32o = w32[:, CT * 3 * C:CT * 3 * C + KT * C].rearrange("p (t o) -> p t o", t=KT)
        ps_s = psum("ps_s", [128, 2, 2, 512])
        ps_a = psum("ps_a", [128, 4, 512])
        class Sem:
            (s_const, s_w, s_wmax, s_wscale, s_whi, s_wlo, s_gn, s_gmm, s_sqrt, s_so, s_ones, s_x,
             s_cur, s_xn, s_xhi, s_xlo, s_qk, s_sig, s_qhi, s_qlo, s_qout, s_stack, s_vps, s_vf,
             s_sq, s_n2, s_n1, s_rn, s_vn, s_vhi, s_vlo, s_s, s_shi, s_slo, s_sm, s_avt, s_av,
             s_avs, s_den, s_rec, s_num, s_o, s_tr, s_othi, s_otlo, s_y, s_ysum, s_ybias, s_yout) = semaphores(
                nc, "a",
                "const w wmax wscale whi wlo gn gmm sqrt so ones x cur xn xhi xlo qk sig qhi qlo "
                "qout stack vps vf sq n2 n1 rn vn vhi vlo s shi slo sm avt av avs den rec num o "
                "tr othi otlo y ysum ybias yout")
        k = Sem
        s_img = [semaphore(nc, f"a_x{b}") for b in range(B)]
        gn.ps_mean, gn.ps_var = ps_a[:, 0, 0:B * CT], ps_a[:, 1, 0:B * CT]
        block = stage_block(nc, c)
        NS = HEADS * NB

        def halves(ps):
            return ps[:, :, 0:HALF]

        def in_two(t):
            return t.rearrange("p (h q) -> p h q", q=HALF)

        @block.sync
        def _(sp):
            sp.dma_start(w32qkv, ins["wqkv"]).then_inc(k.s_w, 16)
            sp.dma_start(w32o, ins["wout"]).then_inc(k.s_w, 16)
            sp.dma_start(bo[:], ins["bout"]).then_inc(k.s_const, 16)
            sp.dma_start(masks[:], ins["masks"]).then_inc(k.s_const, 16)
            for b in range(B):
                if b >= 2:
                    sp.wait_ge(k.s_gn, since(2 * CT * (b - 1)))
                sp.dma_start(xb[:, b % 2].rearrange("p k q -> p (k q)"), x1_d[b]
                             ).then_inc(s_img[b], 16)
            sp.wait_ge(k.s_gn, since(2 * CT * B))
            with sp.Fori(0, B) as b:
                sp.wait_ge(k.s_ysum, since(2 * CT * b))
                sp.dma_start(xb[:, 0].rearrange("p k q -> p (k q)"), x1_d[b]).then_inc(k.s_x, 16)
                for i in range(2):
                    wait_both(sp, (k.s_stack, 192 * b), (k.s_qlo, 2 * CT * b + CT * (i + 1)))
                    sp.dma_start(qk_d[i].rearrange("m p h q -> p m h q"),
                                 qh[:, CT * i:CT * (i + 1)]).then_inc(k.s_qout, 16)
                wait_both(sp, (k.s_qout, 32 * (b + 1)), (k.s_s, NS * b))
                for i, order in enumerate(((0, 0, 1), (0, 1, 0))):
                    for j, h in enumerate(order):
                        for m in range(CT):
                            src = qk_d[i, m].rearrange("(a d) h q -> d a h q", d=HD)[:, :, h, :]
                            sp.dma_start(stacks[HD * j:HD * (j + 1), i, m * 4:(m + 1) * 4, :], src
                                         ).then_inc(k.s_stack, 16)
                sp.wait_ge(k.s_ybias, since(CT * (b + 1)))
                sp.dma_start(out[b].rearrange("(k p) i j -> p k (i j)", p=128), xb[:, 1]
                             ).then_inc(k.s_yout, 16)
            sp.wait_ge(k.s_yout, since(16 * B))

        @block.gpsimd
        def _(pool):
            pool.memset(v[:, :, :, HD:HD + 1], V_UP).then_inc(k.s_ones, 1)
            pool.wait_ge(k.s_wmax, since(4))
            pool.partition_all_reduce(most[:], maxes[:], 128, ABSMAX).then_inc(k.s_wmax, 1)

        NAMES = ("q", "k", "v")

        def used_masked(eng, b, n):
            m = n - 2
            if m < 0:
                eng.wait_ge(k.s_av, since(HEADS * b))
            elif m % NB == NB - 1:
                eng.wait_ge(k.s_av, since(HEADS * b + m // NB + 1))
            else:
                eng.wait_ge(k.s_avt, since((NB - 1) * (HEADS * b + m // NB) + m % NB + 1))

        def sums(act, b, head):
            g = HEADS * b + head
            act.wait_ge(k.s_av, since(g + 1))
            act.wait_ge(k.s_o, since(g))
            flat = av[:].rearrange("p a d -> p (a d)")
            act.activation(flat[:, 0:6 * CW].rearrange("p (x y) -> p x y", y=2 * CW),
                           ps_a[0:BP, 0:3, 0:2 * CW], ACT.Copy).then_inc(k.s_avs, 1)
            act.activation(flat[:, 6 * CW:7 * CW], ps_a[0:BP, 3, 0:CW], ACT.Copy
                           ).then_inc(k.s_avs, 1)

        def attention(dve, b, head):
            g = HEADS * b + head
            dve.wait_ge(k.s_avs, since(2 * g + 2))
            dve.tensor_scalar(rec[:, 0, :], av[:, :, HD], NORM_EPS, None, ALU.add
                              ).then_inc(k.s_den, 1)
            dve.tensor_tensor(num[:], av[:, :, 0:HD], av[:, :, HD + 1:VW], ALU.add
                              ).then_inc(k.s_num, 1)
            dve.wait_ge(k.s_den, since(g + 1))
            dve.reciprocal(rec[:, 1, :], rec[:, 0, :]).then_inc(k.s_rec, 1)
            dve.wait_ge(k.s_rec, since(g + 1))
            dve.wait_ge(k.s_num, since(g + 1))
            dve.wait_ge(k.s_tr, since(2 * KT * b))
            dve.tensor_tensor(o[0:BP, :, head * HD:(head + 1) * HD], num[:],
                              rec[:, 1, :].unsqueeze(2).broadcast_to([BP, NB * NW, HD]),
                              ALU.mult).then_inc(k.s_o, 1)

        @block.vector
        def _(dve):
            dve.wait_ge(k.s_w, since(32))
            for i in range(3):
                dve.tensor_reduce(maxes[:, i:i + 1], w32qkv[:, :, i, :], AX.XY, ALU.max,
                                  apply_absolute_value=True).then_inc(k.s_wmax, 1)
            dve.tensor_reduce(maxes[:, 3:4], w32o, AX.XY, ALU.max, apply_absolute_value=True
                              ).then_inc(k.s_wmax, 1)
            dve.wait_ge(k.s_wmax, since(5))
            a = SCALES["q"]
            power_of_two(dve, k.s_wscale, most[:], kept.scale[:, a:a + 4], kept.inv[:, a:a + 4])
            dve.tensor_scalar(so[:], kept.scale_of("o"), 1 / O_UP, None, ALU.mult).then_inc(k.s_so, 1)
            dve.wait_ge(k.s_so, since(1))
            for i, name in enumerate(NAMES):
                dve.wait_ge(k.s_whi, since(i + 1))
                dve.scalar_tensor_tensor(wqkv[:, 1, :, i, :], w32qkv[:, :, i, :], kept.inv_of(name),
                                         wqkv[:, 0, :, i, :], ALU.mult, ALU.subtract
                                         ).then_inc(k.s_wlo, 1)
            dve.wait_ge(k.s_whi, since(4))
            dve.scalar_tensor_tensor(wo[:, 1], w32o, kept.inv_of("o"), wo[:, 0], ALU.mult,
                                     ALU.subtract).then_inc(k.s_wlo, 1)
            gn_statistics_dve(dve, s_img, lambda ct, b: xb[:, b % 2, ct, :], gn, k)
            dve.wait_ge(k.s_const, since(32))
            dve.wait_ge(k.s_wlo, since(4))
            with dve.Fori(0, B) as b:
                dve.tensor_copy(cur[:], gn.cols[:, bass.ds(b, 1), :].rearrange("p b c -> p (b c)")
                                ).then_inc(k.s_cur, 1)
                dve.wait_ge(k.s_cur, since(b + 1))
                dve.wait_ge(k.s_x, since(16 * (b + 1)))
                for ct in range(CT):
                    dve.tensor_scalar(xn[:, ct, :], xb[:, 0, ct, :], cur[:, ct:ct + 1],
                                      cur[:, CT + ct:CT + ct + 1], ALU.subtract, ALU.mult
                                      ).then_inc(k.s_xn, 1)
                for ct in range(CT):
                    dve.wait_ge(k.s_xhi, since(CT * b + ct + 1))
                    dve.tensor_tensor(xh[:, ct, 1, :], xn[:, ct, :], xh[:, ct, 0, :], ALU.subtract
                                      ).then_inc(k.s_xlo, 1)
                for i in range(2 * CT):
                    dve.wait_ge(k.s_qhi, since(2 * CT * b + i + 1))
                    dve.scalar_tensor_tensor(qh[:, i, 1, :], qf[:, i % 2, :], Q_UP, qh[:, i, 0, :],
                                             ALU.mult, ALU.subtract).then_inc(k.s_qlo, 1)
                dve.wait_ge(k.s_vf, since(NB * (b + 1)))
                dve.wait_ge(k.s_y, since(2 * CT * b))
                flat = vf[:].rearrange("p t c -> p (t c)")
                dve.tensor_tensor(sq, flat, flat, ALU.mult).then_inc(k.s_sq, 1)
                dve.wait_ge(k.s_sq, since(b + 1))
                dve.tensor_reduce(norm[:, 0, :], sq.rearrange("p (h d) -> p h d", d=HD), AX.X,
                                  ALU.add).then_inc(k.s_n2, 1)
                dve.wait_ge(k.s_n1, since(b + 1))
                dve.tensor_scalar(norm[:, 1, :], norm[:, 1, :], 1e-12, None, ALU.max
                                  ).then_inc(k.s_rn, 1)
                dve.wait_ge(k.s_rn, since(2 * b + 1))
                dve.reciprocal(norm[:, 1, :], norm[:, 1, :]).then_inc(k.s_rn, 1)
                dve.wait_ge(k.s_rn, since(2 * b + 2))
                by_head = flat.rearrange("p (h d) -> p h d", d=HD)
                dve.tensor_tensor(by_head, by_head, norm[:, 1, :].unsqueeze(2)
                                  .broadcast_to([BP, NB * HEADS, HD]), ALU.mult).then_inc(k.s_vn, 1)
                vv = v[:].rearrange("p t h d -> p (t h) d")
                dve.wait_ge(k.s_vhi, since(b + 1))
                dve.scalar_tensor_tensor(vv[:, :, HD + 1:VW], by_head, V_UP, vv[:, :, 0:HD],
                                         ALU.mult, ALU.subtract).then_inc(k.s_vlo, 1)
                for n in range(NS):
                    head, t = divmod(n, NB)
                    dve.wait_ge(k.s_shi, since(NS * b + n + 1))
                    dve.scalar_tensor_tensor(in_two(sh[:, n % 2, 1, :]), halves(ps_s[0:BP, n % 2]),
                                             S_DOWN, in_two(sh[:, n % 2, 0, :]), ALU.mult,
                                             ALU.subtract).then_inc(k.s_slo, 1)
                    dve.wait_ge(k.s_slo, since(NS * b + n + 1))
                    used_masked(dve, b, n)
                    for w in range(NW):
                        rs = reached(w, t)
                        a, z = rs[0] * BP, (rs[-1] + 1) * BP
                        m = (rs[0] - t + NB - 1) * BP
                        dve.tensor_tensor(sm[w][:, n % 2, :, 0:z - a], sh[:, n % 2, :, a:z],
                                          masks[:, w, m:m + z - a].unsqueeze(1)
                                          .broadcast_to([BP, 2, z - a]), ALU.mult
                                          ).then_inc(k.s_sm, 1)
                    if t == 1 and head:
                        attention(dve, b, head - 1)
                attention(dve, b, HEADS - 1)
                for kt in range(KT):
                    for i, grp in enumerate(GROUPS):
                        n = 2 * kt + i
                        a, w = grp[0] * BP, len(grp) * BP
                        dve.wait_ge(k.s_othi, since(2 * KT * b + n + 1))
                        dve.scalar_tensor_tensor(ot[:, kt, 1, a:a + w], ps_s[:, kt % 2, i, 0:w],
                                                 O_UP, ot[:, kt, 0, a:a + w], ALU.mult,
                                                 ALU.subtract).then_inc(k.s_otlo, 1)
                dve.wait_ge(k.s_yout, since(16 * b))
                for mt in range(CT):
                    for i, grp in enumerate(GROUPS):
                        a, w = grp[0] * BP, len(grp) * BP
                        dve.wait_ge(k.s_y, since(2 * CT * b + 2 * mt + i + 1))
                        dve.scalar_tensor_tensor(xb[:, 1, mt, a:a + w], ps_a[:, 2 * mt + i, 0:w],
                                                 so[:, 0:1], xb[:, 0, mt, a:a + w], ALU.mult,
                                                 ALU.add).then_inc(k.s_ysum, 1)

        @block.scalar
        def _(act):
            act.wait_ge(k.s_wscale, since(3))
            for i, name in enumerate(NAMES):
                act.activation(wqkv[:, 0, :, i, :], w32qkv[:, :, i, :], ACT.Copy,
                               scale=kept.inv_of(name)).then_inc(k.s_whi, 1)
            act.activation(wo[:, 0], w32o, ACT.Copy, scale=kept.inv_of("o")).then_inc(k.s_whi, 1)
            gn_statistics_act(act, gn, k)
            act.wait_ge(k.s_const, since(32))
            with act.Fori(0, B) as b:
                for ct in range(CT):
                    act.wait_ge(k.s_xn, since(CT * b + ct + 1))
                    act.activation(xh[:, ct, 0, :], xn[:, ct, :], ACT.Copy).then_inc(k.s_xhi, 1)
                act.wait_ge(k.s_qout, since(32 * b))
                for i in range(2 * CT):
                    act.wait_ge(k.s_qk, since(2 * CT * b + i + 1))
                    act.wait_ge(k.s_qlo, since(earlier(b, i, 2, 2 * CT)))
                    act.activation(in_two(qf[:, i % 2, :]), halves(ps_s[:, i % 2]), ACT.Sigmoid,
                                   scale=kept.scale_of(NAMES[i // CT])).then_inc(k.s_sig, 1)
                    act.wait_ge(k.s_sig, since(2 * CT * b + i + 1))
                    act.activation(qh[:, i, 0, :], qf[:, i % 2, :], ACT.Copy, scale=Q_UP
                                   ).then_inc(k.s_qhi, 1)
                act.wait_ge(k.s_vlo, since(b))
                for t in range(NB):
                    act.wait_ge(k.s_vps, since(NB * b + t + 1))
                    act.activation(vf[:, t, :], ps_a[0:BP, t % 4, 0:C], ACT.Copy,
                                   scale=kept.scale_of("v", BP)).then_inc(k.s_vf, 1)
                act.wait_ge(k.s_n2, since(b + 1))
                act.activation(norm[:, 1, :], norm[:, 0, :], ACT.Sqrt).then_inc(k.s_n1, 1)
                act.wait_ge(k.s_vn, since(b + 1))
                act.wait_ge(k.s_av, since(HEADS * b))
                act.activation(v[:].rearrange("p t h d -> p (t h) d")[:, :, 0:HD],
                               vf[:].rearrange("p t (h d) -> p (t h) d", d=HD), ACT.Copy, scale=V_UP
                               ).then_inc(k.s_vhi, 1)
                for n in range(NS):
                    head, t = divmod(n, NB)
                    act.wait_ge(k.s_s, since(NS * b + n + 1))
                    act.wait_ge(k.s_sm, since(NW * earlier(b, n, 2, NS)))
                    act.activation(in_two(sh[:, n % 2, 0, :]), halves(ps_s[0:BP, n % 2]), ACT.Copy,
                                   scale=S_DOWN).then_inc(k.s_shi, 1)
                    if t == 1 and head:
                        sums(act, b, head - 1)
                sums(act, b, HEADS - 1)
                for kt in range(KT):
                    for i, grp in enumerate(GROUPS):
                        n = 2 * kt + i
                        a, w = grp[0] * BP, len(grp) * BP
                        act.wait_ge(k.s_tr, since(2 * KT * b + n + 1))
                        act.activation(ot[:, kt, 0, a:a + w], ps_s[:, kt % 2, i, 0:w], ACT.Copy,
                                       scale=O_UP).then_inc(k.s_othi, 1)
                for mt in range(CT):
                    act.wait_ge(k.s_ysum, since(2 * CT * b + 2 * mt + 2))
                    act.activation(xb[:, 1, mt, :], xb[:, 1, mt, :], ACT.Identity,
                                   bias=bo[:, mt:mt + 1]).then_inc(k.s_ybias, 1)

        @block.tensor
        def _(pe):
            gn_statistics_pe(pe, kept.grp, gn, k)
            pe.wait_ge(k.s_wlo, since(4))

            def scores(b, n):
                head, t = divmod(n, NB)
                pe.wait_ge(k.s_slo, since(earlier(b, n, 2, NS)))
                for h in range(2):
                    mm = pe.matmul(ps_s[0:BP, n % 2, h, 0:HALF],
                                   stacks[:, 1, head, t * BP:(t + 1) * BP],
                                   stacks[:, 0, head, h * HALF:(h + 1) * HALF], start=True, stop=True)
                mm.then_inc(k.s_s, 1)

            with pe.Fori(0, B) as b:
                pe.wait_ge(k.s_xlo, since(CT * (b + 1)))
                pe.wait_ge(k.s_otlo, since(2 * KT * b))
                for i in range(2 * CT):
                    pe.wait_ge(k.s_qhi, since(earlier(b, i, 2, 2 * CT)))
                    which, mt = divmod(i, CT)
                    for h in range(2):
                        for ct in range(CT):
                            mm = three_passes(
                                pe, ps_s[:, i % 2, h, 0:HALF],
                                lambda a: wqkv[:, a, ct, which, mt * 128:(mt + 1) * 128],
                                lambda a: xh[:, ct, a, h * HALF:(h + 1) * HALF], ct == 0,
                                ct == CT - 1)
                    mm.then_inc(k.s_qk, 1)
                pe.wait_ge(k.s_ysum, since(2 * CT * b))
                for t in range(NB):
                    pe.wait_ge(k.s_vf, since(earlier(b, t, 4, NB)))
                    for ct in range(CT):
                        mm = three_passes(pe, ps_a[0:BP, t % 4, 0:C],
                                          lambda a: xh[:, ct, a, t * BP:(t + 1) * BP],
                                          lambda a: wqkv[:, a, ct, 2, :], ct == 0, ct == CT - 1)
                    mm.then_inc(k.s_vps, 1)
                pe.wait_ge(k.s_stack, since(192 * (b + 1)))
                pe.wait_ge(k.s_qlo, since(2 * CT * (b + 1)))
                pe.wait_ge(k.s_vf, since(NB * (b + 1)))
                pe.wait_ge(k.s_vlo, since(b + 1))
                scores(b, 0)
                for n in range(NS):
                    head, t = divmod(n, NB)
                    if n + 1 < NS:
                        scores(b, n + 1)
                    if t == 0:
                        begun = set()
                        if head:
                            pe.wait_ge(k.s_avs, since(2 * (HEADS * b + head)))
                    for w in range(NW):
                        pe.wait_ge(k.s_sm, since(NW * (NS * b + n) + w + 1))
                        rs = reached(w, t)
                        for r in rs:
                            at = (r % 2) * CW + w * VW
                            for h, cols in ((0, VW), (1, HD + 1)):
                                mm = pe.matmul(ps_a[0:BP, r // 2, at:at + cols],
                                               sm[w][:, n % 2, h, (r - rs[0]) * BP:
                                                     (r - rs[0] + 1) * BP],
                                               v[:, t, head, 0:cols], start=r // 2 not in begun,
                                               stop=True, skip_group_check=True)
                                begun.add(r // 2)
                    mm.then_inc(k.s_avt if t < NB - 1 else k.s_av, 1)
                for kt in range(KT):
                    pe.wait_ge(k.s_o, since(HEADS * (b + 1)))
                    pe.wait_ge(k.s_otlo, since(2 * KT * b + max(0, 2 * (kt - 1))))
                    for i, grp in enumerate(GROUPS):
                        for j, r in enumerate(grp):
                            w, ct = divmod(kt, CT)
                            mm = pe.transpose(ps_s[:, kt % 2, i, j * BP:(j + 1) * BP],
                                              o[0:BP, r * NW + w, ct * 128:(ct + 1) * 128],
                                              kept.ident[0:BP, 0:BP])
                        mm.then_inc(k.s_tr, 1)
                pe.wait_ge(k.s_otlo, since(2 * KT * (b + 1)))
                pe.wait_ge(k.s_avs, since(2 * HEADS * (b + 1)))
                for mt in range(CT):
                    for i, grp in enumerate(GROUPS):
                        a, w = grp[0] * BP, len(grp) * BP
                        for kt in range(KT):
                            mm = three_passes(pe, ps_a[:, 2 * mt + i, 0:w],
                                              lambda a_: wo[:, a_, kt, mt * 128:(mt + 1) * 128],
                                              lambda a_: ot[:, kt, a_, a:a + w], kt == 0,
                                              kt == KT - 1)
                        mm.then_inc(k.s_y, 1)


def build(nc, ins, out, upto=9, shown=()):
    def dram(name, shape, dt=F32):
        kind = {"kind": "ExternalOutput"} if name in shown else {}
        return nc.dram_tensor(name, shape, dt, **kind).ap()

    xT_d = dram("xT_d", [B, BP, NB * 2 * C], F16)
    pos1_d = dram("pos1_d", [B, NB, OFF * BP])
    pos2_d = dram("pos2_d", [B, NB, OFF * BP])
    h_d = dram("h_d", [B, NB, 128, HT * BP])
    x1_d = dram("x1_d", [B, 128, CT * PIX])
    q_d = dram("q_d", [2, CT, 128, 2, PIX], F16)
    def stage(number, run, *args):
        if number <= upto:
            before = nc.snapshot_sems()
            run(nc, kept, *args)
            nc.clear_and_free_semaphores(nc.allocated_since(before))
            nc.all_engine_barrier()

    with ExitStack() as ctx:
        kept = Kept(nc, ctx)
        with ExitStack() as c:
            wts = Weights(nc, c)
            stage(1, stage_norm, wts, ins["x"], ins["w1"], ins["woff1"], ins["boff1"], ins, xT_d,
                  pos1_d)
            stage(2, stage_layer1, wts, xT_d, pos1_d, h_d)
            stage(3, stage_offsets2, wts, ins["w2"], ins["woff2"], ins["boff2"], ins, h_d, pos2_d)
            stage(4, stage_layer2, wts, h_d, pos2_d, ins["x"], x1_d)
        stage(5, stage_attention, ins, x1_d, q_d, out)


def launch_arrays(x, w_p1, b_p1, w_m1, b_m1, w_c1, w_p2, b_p2, w_m2, b_m2, w_c2, Wq, Wk, Wv, Wout, bout):
    def offsets(w_p, w_m):
        w = np.concatenate([w_p, w_m], 0).reshape(OFF, -1, 128, TAPS)
        return np.ascontiguousarray(w.transpose(2, 1, 3, 0)).reshape(128, -1, OFF)

    first = w_c1.reshape(HID, CT, 128, TAPS).transpose(2, 1, 3, 0).reshape(128, -1)
    second = w_c2.reshape(C, HT, 128, TAPS).transpose(2, 3, 1, 0)
    pairs = second[:, :8].reshape(128, 4, 2, HT, C).transpose(0, 1, 3, 2, 4).reshape(128, -1)
    second = np.concatenate([pairs, second[:, 8].reshape(128, -1)], 1)
    qkv = np.stack([w.T for w in (Wq, Wk, Wv)], 0).reshape(3, CT, 128, C).transpose(2, 1, 0, 3)
    o = Wout.T.reshape(len(WINDOWS) * CT, 128, C).transpose(1, 0, 2)
    return {
        "x": x, "w1": first, "woff1": offsets(w_p1, w_m1),
        "boff1": np.concatenate([b_p1, b_m1])[:, None], "w2": second, "woff2": offsets(w_p2, w_m2),
        "boff2": np.concatenate([b_p2, b_m2])[:, None], "wqkv": qkv, "wout": o,
        "bout": bout.reshape(CT, 128).T,
    }


def kernel(**inputs):
    import concourse.bacc as bacc
    from concourse.bass_utils import run_bass_kernel_spmd

    given = {n.replace("L0_conv_", "").replace("L1_conv_", ""): np.asarray(a) for n, a in inputs.items()}
    arrays = launch_arrays(**given) | constants()
    arrays = {f"in_{n}": np.ascontiguousarray(a) for n, a in arrays.items()}
    nc = bacc.Bacc("TRN2", target_bir_lowering=False, num_devices=1)
    ins = {n[3:]: nc.dram_tensor(n, a.shape, mybir.dt.from_np(a.dtype), kind="ExternalInput").ap()
           for n, a in arrays.items()}
    out = nc.dram_tensor("out", (B, C, S, S), F32, kind="ExternalOutput").ap()
    build(nc, ins, out)
    got = run_bass_kernel_spmd(nc, [arrays], core_ids=[0])
    return got.results[0]["out"]
```

```python
from contextlib import ExitStack

import numpy as np

import concourse.bass as bass
from concourse import mybir

ALU = mybir.AluOpType
ACT = mybir.ActivationFunctionType
F32 = mybir.dt.float32
F16 = mybir.dt.float16
I32 = mybir.dt.int32
AX = mybir.AxisListType
ABSMAX = bass.bass_isa.ReduceOp.absmax

B, C, HID, S = 8, 256, 1024, 28
PIX = S * S
TAPS = 9
OFF = 3 * TAPS
RB = 4
BP = RB * S
NB = S // RB
JW = TAPS * BP
CT = C // 128
HT = HID // 128
GROUPS = (tuple(range(0, 4)), tuple(range(4, NB)))
PADW = S + 2
PADN = PADW * PADW
HALF = PIX // 2
FAR = 2.999
GN_EPS = 1e-5
HEADS, HD = 8, 32
WINDOWS = (1, 2, 4)
VW = 2 * HD + 1
Q_UP, S_DOWN, V_UP, O_UP = 2.0 ** 15, 2.0 ** -20, 2.0 ** 8, 2.0 ** 10
NORM_EPS = 1e-6 * Q_UP * Q_UP * S_DOWN * V_UP
W_SLOTS, W_SLOT = 18, 1024
W_LAG = 2
LO_HI = ((0, 0), (1, 0), (0, 1))


def group_of(r):
    return 0 if r in GROUPS[0] else 1


def window_blocks(ws):
    up = (ws - 1) - (ws - 1) // 2
    down = ws - 1 - up
    return -((RB - 1 + down) // RB), (RB - 1 + up) // RB


def constants():
    p = np.arange(128)
    ident = np.eye(128, dtype=np.float32)
    grp = (p[:, None] // 8 == p[None, :] // 8).astype(np.float32) / 8
    sel = ((p[:, None] % 32) == np.arange(OFF)[None]).astype(np.float32)
    n, i, j = np.meshgrid(np.arange(TAPS), np.arange(S), np.arange(S), indexing="ij")
    p0n = np.zeros((OFF, PIX), np.float32)
    p0n[:TAPS] = (i + n // 3 - 1).reshape(TAPS, PIX)
    p0n[TAPS:2 * TAPS] = (j + n % 3 - 1).reshape(TAPS, PIX)
    k = np.arange(OFF)
    rows = np.stack([k < 2 * TAPS, k >= 2 * TAPS, k < TAPS], 1).astype(np.float32)
    q = np.arange(BP)
    negq = np.stack([-(RB * t + q // S) for t in range(NB)] + [-(q % S)], 1).astype(np.float32)
    masks = np.zeros((BP, len(WINDOWS), 2 * NB - 1, RB, S), np.float16)
    for w, div in enumerate(WINDOWS):
        ws = S // div
        up = (ws - 1) - (ws - 1) // 2
        down = ws - 1 - up
        for d in range(2 * NB - 1):
            row = (RB * (d - NB + 1) + np.arange(RB))[None] - (q // S)[:, None]
            col = np.arange(S)[None] - (q % S)[:, None]
            ok = lambda x: (x >= -down) & (x <= up)
            masks[:, w, d] = ok(row)[:, :, None] & ok(col)[:, None, :]
    return {"ident": ident, "grp": grp, "sel": sel, "p0n": p0n, "rows": rows, "negq": negq,
            "masks": masks.reshape(BP, len(WINDOWS), -1)}


START = 1


def since(count):
    return count + START


def power_of_two(dve, sem, most, scale, inverse):
    def as_int(t):
        return t.bitcast(I32)
    dve.tensor_scalar(most, most, 1e-30, None, ALU.max).then_inc(sem, 1)
    dve.wait_ge(sem, since(1))
    dve.tensor_scalar(as_int(scale), as_int(most), 0x7F800000, None, ALU.bitwise_and).then_inc(sem, 1)
    dve.wait_ge(sem, since(2))
    dve.tensor_scalar(as_int(inverse), as_int(scale), -1.0, float(0x7F000000), ALU.mult, ALU.add
                      ).then_inc(sem, 1)
    dve.wait_ge(sem, since(3))


def three_passes(pe, out, lhs, rhs, start, stop):
    for i, (a, b) in enumerate(LO_HI):
        mm = pe.matmul(out, lhs(a), rhs(b), start=start and i == 0, stop=stop and i == 2,
                       skip_group_check=True)
    return mm



GN_STEPS = B * CT


def gn_buffers(sb, given=None):
    class Gn:
        stats = sb("stats", [128, B * CT, 2, 6]) if given is None else given
        agg = sb("agg", [128, B * CT, 2])
        means, dev, var = (sb(n, [128, B * CT]) for n in ("means", "dev", "var"))
        cols = sb("cols", [128, B, 2 * CT])
    return Gn


def gn_statistics_dve(dve, s_img, img, gn, k):
    for b in range(B):
        dve.wait_ge(s_img[b], since(16))
        for ct in range(CT):
            for h in range(2):
                dve.bn_stats(gn.stats[:, b * CT + ct, h, :],
                             img(ct, b)[:, h * HALF:(h + 1) * HALF]).then_inc(k.s_bn, 1)
    dve.wait_ge(k.s_bn, since(2 * CT * B))
    gn_groups_dve(dve, gn, k)


def gn_groups_dve(dve, gn, k):
    n = B * CT
    for i in range(B * CT):
        dve.bn_aggr(gn.agg[:, i, :], gn.stats[:, i, :, :]).then_inc(k.s_gn, 1)
    dve.wait_ge(k.s_gn, since(n))
    dve.tensor_copy(gn.means[:], gn.agg[:, :, 0]).then_inc(k.s_gn, 1)
    dve.wait_ge(k.s_gmm, since(1))
    by_image = gn.cols[:, :, 0:CT]
    dve.tensor_copy(by_image, gn.ps_mean.rearrange("p (b c) -> p b c", c=CT)).then_inc(k.s_gn, 1)
    dve.wait_ge(k.s_gn, since(n + 2))
    dev = gn.dev[:].rearrange("p (b c) -> p b c", c=CT)
    dve.tensor_tensor(dev, gn.means[:].rearrange("p (b c) -> p b c", c=CT), by_image, ALU.subtract
                      ).then_inc(k.s_gn, 1)
    dve.wait_ge(k.s_gn, since(n + 3))
    dve.tensor_tensor(gn.dev[:], gn.dev[:], gn.dev[:], ALU.mult).then_inc(k.s_gn, 1)
    dve.wait_ge(k.s_gn, since(n + 4))
    dve.tensor_tensor(gn.var[:], gn.agg[:, :, 1], gn.dev[:], ALU.add).then_inc(k.s_gn, 1)
    dve.wait_ge(k.s_gmm, since(2))
    dve.tensor_scalar(gn.var[:], gn.ps_var, GN_EPS, None, ALU.add).then_inc(k.s_gn, 1)
    dve.wait_ge(k.s_sqrt, since(1))
    dve.reciprocal(gn.cols[:, :, CT:2 * CT], dev).then_inc(k.s_gn, 1)
    dve.wait_ge(k.s_gn, since(n + 7))


def gn_statistics_pe(pe, grp, gn, k):
    pe.wait_ge(k.s_gn, since(GN_STEPS + 1))
    pe.matmul(gn.ps_mean, grp[:], gn.means[:], start=True, stop=True).then_inc(k.s_gmm, 1)
    pe.wait_ge(k.s_gn, since(GN_STEPS + 5))
    pe.matmul(gn.ps_var, grp[:], gn.var[:], start=True, stop=True).then_inc(k.s_gmm, 1)


def gn_statistics_act(act, gn, k):
    act.wait_ge(k.s_gn, since(GN_STEPS + 6))
    act.activation(gn.dev[:], gn.var[:], ACT.Sqrt).then_inc(k.s_sqrt, 1)



def offset_conv_pe(pe, ps, w, xp, tiles):
    steps = [(kt, n, a, b) for kt in range(tiles) for n in range(TAPS) for a, b in LO_HI]
    for half in range(2):
        for i, (kt, n, a, b) in enumerate(steps):
            g = i % 4
            top = n // 3 + half * (S // 2)
            mm = pe.matmul(ps[32 * g:32 * g + 32, half, 0:HALF], w(kt, n, a),
                           xp(kt, b)[:, top:top + S // 2, n % 3:n % 3 + S], start=i < 4,
                           stop=i >= len(steps) - 4, skip_group_check=True)
    return mm


def offsets_act(act, b, psA, psB, quarters, scale, bias, offs, msk, k):
    act.wait_ge(k.s_conv, since(b + 1))
    act.wait_ge(k.s_sum, since(2 * b))
    for h in range(2):
        act.activation(quarters[:, h, :], psA[:, h, 0:HALF], ACT.Copy).then_inc(k.s_quarters, 1)
    act.wait_ge(k.s_pos, since(2 * b))
    act.wait_ge(k.s_reach, since(b))
    for h in range(2):
        act.wait_ge(k.s_sum, since(2 * b + h + 1))
        act.activation(offs[:, h, :], psB[0:OFF, h, 0:HALF], ACT.Identity, bias=bias[:, 0:1],
                       scale=scale).then_inc(k.s_offs, 1)
    act.wait_ge(k.s_posout, since(32 * b))
    for h in range(2):
        act.activation(msk[:, h, :], psB[0:OFF, h, 0:HALF], ACT.Sigmoid, bias=bias[:, 0:1],
                       scale=scale).then_inc(k.s_msk, 1)


def positions_dve(dve, b, offs, p0n, pos, reach, k):
    dve.wait_ge(k.s_posout, since(32 * b))
    for h in range(2):
        dve.wait_ge(k.s_offs, since(2 * b + h + 1))
        dve.tensor_tensor(pos[:, h, :], offs[:, h, :], p0n[:, h * HALF:(h + 1) * HALF],
                          ALU.add).then_inc(k.s_pos, 1)
    dve.tensor_reduce(reach[0:OFF, bass.ds(b, 1)], offs[:], AX.XY, ALU.max,
                      apply_absolute_value=True).then_inc(k.s_reach, 1)


def sum_quarters_pe(pe, b, psB, sel, quarters, k):
    pe.wait_ge(k.s_offs, since(2 * b))
    pe.wait_ge(k.s_msk, since(2 * b))
    for h in range(2):
        pe.wait_ge(k.s_quarters, since(2 * b + h + 1))
        pe.matmul(psB[0:OFF, h, 0:HALF], sel[:], quarters[:, h, :], start=True, stop=True
                  ).then_inc(k.s_sum, 1)


def store_positions_sp(sp, b, to, pos, msk, k):
    sp.wait_ge(k.s_pos, since(2 * (b + 1)))
    sp.wait_ge(k.s_msk, since(2 * (b + 1)))
    to = to.rearrange("r (k q) -> k r q", q=BP)
    view = lambda t: t[:].rearrange("k h q -> k (h q)").rearrange("k (r q) -> k r q", q=BP)
    sp.dma_start(to[0:2 * TAPS], view(pos)[0:2 * TAPS]).then_inc(k.s_posout, 16)
    sp.dma_start(to[2 * TAPS:OFF], view(msk)[2 * TAPS:OFF]).then_inc(k.s_posout, 16)


def far_flag_dve(dve, reach, rows, flag, k):
    dve.wait_ge(k.s_reach, since(B))
    dve.tensor_reduce(reach[:, B:B + 1], reach[:, 0:B], AX.X, ALU.max).then_inc(k.s_far, 1)
    dve.wait_ge(k.s_far, since(1))
    dve.tensor_scalar(reach[0:OFF, B:B + 1], reach[0:OFF, B:B + 1], rows[:, 2:3], None, ALU.mult
                      ).then_inc(k.s_far, 1)
    dve.wait_ge(k.s_far, since(3))
    dve.tensor_scalar(flag, reach[:, B + 1:B + 2], FAR, None, ALU.is_gt).then_inc(k.s_far, 1)


def far_flag_pool(pool, reach, k):
    pool.wait_ge(k.s_far, since(2))
    pool.partition_all_reduce(reach[:, B + 1:B + 2], reach[:, B:B + 1], 128, ABSMAX
                              ).then_inc(k.s_far, 1)


def semaphore(nc, name):
    s = nc.alloc_semaphore(name)
    nc.gpsimd.sem_inc(s, START)
    return s


def stage_block(nc, c):
    nc.all_engine_barrier()
    return c.enter_context(nc.Block())


def semaphores(nc, stage, names):
    return [semaphore(nc, f"{stage}_{n}") for n in names.split()]


SCALES = {"w1": 0, "p1": 1, "m1": 2, "w2": 3, "p2": 4, "m2": 5, "h": 6, "q": 7, "k": 8, "v": 9, "o": 10}


class Kept:

    def __init__(self, nc, ctx):
        def sb(name, shape, dt=F32):
            return ctx.enter_context(nc.sbuf_tensor(name, shape, dt))
        self.ident = sb("ident_s", [128, 128])
        self.grp = sb("grp_s", [128, 128])
        self.sel = sb("sel_s", [128, OFF])
        self.negq = sb("negq_s", [BP, NB + 1])
        self.rows = sb("rows_s", [OFF, 3])
        self.scale = sb("scale_w", [128, len(SCALES)])
        self.inv = sb("inv_w", [128, len(SCALES)])
        self.stats = sb("stats_x1", [128, B * CT, 2, 6])
        self.hmax = sb("hmax", [128, 2])
        self.far = sb("far", [128, 2], I32)

    def scale_of(self, name, parts=128):
        return self.scale[0:parts, SCALES[name]:SCALES[name] + 1]

    def inv_of(self, name, parts=128):
        return self.inv[0:parts, SCALES[name]:SCALES[name] + 1]


class Weights:

    def __init__(self, nc, ctx):
        self.big = ctx.enter_context(nc.sbuf_tensor("weights", [128, W_SLOTS + W_LAG, 2 * W_SLOT], F16))

    def words(self, c):
        return self.big[:, c, :].bitcast(F32)

    def half(self, c, h):
        return self.big[:, c, h * W_SLOT:(h + 1) * W_SLOT]

    def load(self, sp, src, k):
        for c in range(W_SLOTS):
            sp.dma_start(self.words(c + W_LAG), src[:, c * W_SLOT:(c + 1) * W_SLOT]).then_inc(k.s_w, 16)

    def largest(self, dve, maxes, k, part, parts):
        n = W_SLOTS * W_SLOT // parts
        flat = self.big[:].rearrange("p c j -> p (c j)").bitcast(F32)
        dve.wait_ge(k.s_w, since(16 * W_SLOTS))
        dve.tensor_reduce(maxes[:, bass.ds(part, 1)], flat[:, bass.ds(part * n + W_LAG * W_SLOT, n)], AX.X,
                          ALU.max, apply_absolute_value=True).then_inc(k.s_wmax, 1)

    def largest_of_parts(self, dve, maxes, k, parts):
        dve.wait_ge(k.s_wmax, since(parts))
        dve.tensor_reduce(maxes[:, W_SLOTS:W_SLOTS + 1], maxes[:, 0:parts], AX.X, ALU.max
                          ).then_inc(k.s_wmax, 1)

    def split_high(self, act, inv, k):
        act.wait_ge(k.s_wscale, since(3))
        for c in range(W_SLOTS):
            if c >= W_LAG:
                act.wait_ge(k.s_wlo, since(c - W_LAG + 1))
            act.activation(self.half(c, 0), self.words(c + W_LAG), ACT.Copy, scale=inv
                           ).then_inc(k.s_whi, 1)

    def split_low(self, dve, inv, k):
        for c in range(W_SLOTS):
            dve.wait_ge(k.s_whi, since(c + 1))
            dve.scalar_tensor_tensor(self.half(c, 1), self.words(c + W_LAG), inv, self.half(c, 0),
                                     ALU.mult, ALU.subtract).then_inc(k.s_wlo, 1)


def largest_weight_pool(pool, maxes, most, k, parts):
    pool.wait_ge(k.s_wmax, since(parts + 1))
    pool.partition_all_reduce(most[:], maxes[:, W_SLOTS:W_SLOTS + 1], 128, ABSMAX
                              ).then_inc(k.s_wmax, 1)


def offset_weights_dve(dve, wo32, wo, maxes2, most2, osc, kept, k, p, m, extra=None):
    dve.wait_ge(k.s_wo, since(16))
    for i, (a, z) in enumerate(((0, 2 * TAPS), (2 * TAPS, OFF))):
        dve.tensor_reduce(maxes2[:, i:i + 1], wo32[:, :, a:z], AX.XY, ALU.max,
                          apply_absolute_value=True).then_inc(k.s_womax, 1)
    dve.wait_ge(k.s_womax, since(3))
    i = SCALES[p]
    power_of_two(dve, k.s_woscale, most2[:], kept.scale[:, i:i + 2], kept.inv[:, i:i + 2])
    dve.tensor_scalar(osc[:, 0:1], kept.rows[:, 0:1], kept.scale_of(p, OFF), None, ALU.mult
                      ).then_inc(k.s_osc, 1)
    dve.wait_ge(k.s_osc, since(1))
    dve.scalar_tensor_tensor(osc[:, 1:2], kept.rows[:, 1:2], kept.scale_of(m, OFF), osc[:, 0:1],
                             ALU.mult, ALU.add).then_inc(k.s_osc, 1)
    dve.wait_ge(k.s_osc, since(2))
    if extra is not None:
        dve.tensor_scalar(osc[:, 1:2], osc[:, 1:2], extra, None, ALU.mult).then_inc(k.s_osc, 1)
    dve.wait_ge(k.s_wohi, since(2))
    for a, z, name in ((0, 2 * TAPS, p), (2 * TAPS, OFF, m)):
        dve.scalar_tensor_tensor(wo[:, 1, :, a:z], wo32[:, :, a:z], kept.inv_of(name),
                                 wo[:, 0, :, a:z], ALU.mult, ALU.subtract).then_inc(k.s_wolo, 1)


def offset_weights_pool(pool, maxes2, most2, k):
    pool.wait_ge(k.s_womax, since(2))
    pool.partition_all_reduce(most2[:], maxes2[:], 128, ABSMAX).then_inc(k.s_womax, 1)


def offset_weights_act(act, wo32, wo, kept, k, p, m):
    act.wait_ge(k.s_zero, since(1))
    act.wait_ge(k.s_woscale, since(3))
    for a, z, name in ((0, 2 * TAPS, p), (2 * TAPS, OFF, m)):
        act.activation(wo[:, 0, :, a:z], wo32[:, :, a:z], ACT.Copy, scale=kept.inv_of(name)
                       ).then_inc(k.s_wohi, 1)



TWOS = [slice(t, min(t + 2, NB)) for t in range(0, NB, 2)]


def two(ps, i, ts):
    return ps[:, i, 0:(ts.stop - ts.start) * C].rearrange("p (t c) -> p t c", c=C)


def stage_norm(nc, kept, wts, x, w1, woff1, boff1, consts, xT_d, pos_d):
    with ExitStack() as c:
        def sb(name, shape, dt=F32):
            return c.enter_context(nc.sbuf_tensor("n_" + name, shape, dt))

        def psum(name, shape, dt=F32):
            return c.enter_context(nc.psum_tensor("n_" + name, shape, dt))

        xs = sb("x", [128, CT, B, PIX])
        xn = sb("xn", [128, CT, PIX])
        xp = sb("xp", [128, CT, 2, PADW, PADW], F16)
        xt = sb("xt", [BP, NB, 2, C], F16)
        gn = gn_buffers(sb)
        cur = sb("cur", [128, 2 * CT])
        wo32 = sb("wo32", [128, CT * TAPS, OFF])
        wo = sb("wo", [128, 2, CT * TAPS, 32], F16)
        maxes, most = sb("maxes", [128, W_SLOTS + 1]), sb("most", [128, 1])
        maxes2, most2 = sb("maxes2", [128, 2]), sb("most2", [128, 2])
        bo, osc = sb("bo", [OFF, 1]), sb("osc", [OFF, 2])
        p0n = sb("p0n", [OFF, PIX])
        quarters = sb("quarters", [128, 2, HALF])
        offs, pos, msk = (sb(n, [OFF, 2, HALF]) for n in ("offs", "pos", "msk"))
        reach = sb("reach", [128, B + 2])
        psA, psB = psum("psA", [128, 2, 512]), psum("psB", [128, 2, 512])
        psT = psum("psT", [BP, 4, 512])
        class Sem:
            (s_const, s_wo, s_w, s_bn, s_gn, s_gmm, s_sqrt, s_womax, s_woscale, s_wohi, s_wolo, s_osc,
             s_wmax, s_wscale, s_whi, s_wlo, s_zero, s_cur, s_xn, s_xphi, s_xplo, s_tr, s_xthi,
             s_xtlo, s_xtout, s_conv, s_quarters, s_sum, s_pos, s_msk, s_offs, s_reach, s_posout,
             s_far) = semaphores(
                nc, "n",
                "const wo w bn gn gmm sqrt womax woscale wohi wolo osc wmax wscale whi wlo zero cur "
                "xn xphi xplo tr xthi xtlo xtout conv quarters sum pos msk offs reach posout far")
        k = Sem
        s_img = [semaphore(nc, f"n_x{b}") for b in range(B)]
        gn.ps_mean, gn.ps_var = psA[:, 0, 0:B * CT], psA[:, 1, 0:B * CT]
        block = stage_block(nc, c)

        @block.sync
        def _(sp):
            for t, name in ((kept.grp, "grp"), (kept.ident, "ident"), (kept.sel, "sel"),
                            (kept.negq, "negq"), (kept.rows, "rows"), (p0n, "p0n")):
                sp.dma_start(t[:], consts[name]).then_inc(k.s_const, 16)
            sp.dma_start(bo[:], boff1).then_inc(k.s_const, 16)
            sp.dma_start(wo32[:], woff1).then_inc(k.s_wo, 16)
            for b in range(B):
                sp.dma_start(xs[:, :, b, :], x[b].rearrange("(k p) i j -> p k (i j)", p=128)
                             ).then_inc(s_img[b], 16)
            wts.load(sp, w1, k)
            with sp.Fori(0, B) as b:
                sp.wait_ge(k.s_xthi, since(len(TWOS) * (b + 1)))
                sp.wait_ge(k.s_xtlo, since(len(TWOS) * (b + 1)))
                sp.dma_start(xT_d[b], xt[:].rearrange("p t h c -> p (t h c)")).then_inc(k.s_xtout, 16)
                store_positions_sp(sp, b, pos_d[b], pos, msk, k)
            sp.wait_ge(k.s_xtout, since(16 * B))
            sp.wait_ge(k.s_posout, since(32 * B))

        @block.gpsimd
        def _(pool):
            pool.memset(wo[:], 0.0).then_inc(k.s_zero, 1)
            pool.memset(xp[:], 0.0).then_inc(k.s_zero, 1)
            pool.memset(reach[:], 0.0).then_inc(k.s_zero, 1)
            offset_weights_pool(pool, maxes2, most2, k)
            largest_weight_pool(pool, maxes, most, k, B)
            far_flag_pool(pool, reach, k)

        @block.vector
        def _(dve):
            dve.wait_ge(k.s_const, since(16 * 7))
            offset_weights_dve(dve, wo32, wo, maxes2, most2, osc, kept, k, "p1", "m1")
            gn_statistics_dve(dve, s_img, lambda ct, b: xs[:, ct, b, :], gn, k)
            dve.wait_ge(k.s_zero, since(3))
            with dve.Fori(0, B) as b:
                dve.tensor_copy(cur[:], gn.cols[:, bass.ds(b, 1), :].rearrange("p b c -> p (b c)")
                                ).then_inc(k.s_cur, 1)
                dve.wait_ge(k.s_cur, since(b + 1))
                dve.wait_ge(k.s_tr, since(len(TWOS) * b))
                dve.wait_ge(k.s_xphi, since(CT * b))
                for ct in range(CT):
                    img = xs[:, ct, bass.ds(b, 1), :].rearrange("p b q -> p (b q)")
                    dve.tensor_scalar(xn[:, ct, :], img, cur[:, ct:ct + 1],
                                      cur[:, CT + ct:CT + ct + 1], ALU.subtract, ALU.mult
                                      ).then_inc(k.s_xn, 1)
                for ct in range(CT):
                    dve.wait_ge(k.s_xphi, since(CT * b + ct + 1))
                    dve.tensor_tensor(xp[:, ct, 1, 1:1 + S, 1:1 + S],
                                      xn[:, ct, :].rearrange("p (i j) -> p i j", j=S),
                                      xp[:, ct, 0, 1:1 + S, 1:1 + S], ALU.subtract
                                      ).then_inc(k.s_xplo, 1)
                for i, ts in enumerate(TWOS):
                    dve.wait_ge(k.s_xthi, since(len(TWOS) * b + i + 1))
                    dve.tensor_tensor(xt[:, ts, 1, :], two(psT, i, ts), xt[:, ts, 0, :],
                                      ALU.subtract).then_inc(k.s_xtlo, 1)
                wts.largest(dve, maxes, k, b, B)
                positions_dve(dve, b, offs, p0n, pos, reach, k)
            wts.largest_of_parts(dve, maxes, k, B)
            far_flag_dve(dve, reach, kept.rows, kept.far[:, 0:1], k)
            dve.wait_ge(k.s_wmax, since(B + 2))
            power_of_two(dve, k.s_wscale, most[:], kept.scale_of("w1"), kept.inv_of("w1"))
            wts.split_low(dve, kept.inv_of("w1"), k)

        @block.scalar
        def _(act):
            offset_weights_act(act, wo32, wo, kept, k, "p1", "m1")
            gn_statistics_act(act, gn, k)
            act.wait_ge(k.s_zero, since(3))
            act.wait_ge(k.s_const, since(16 * 7))
            act.wait_ge(k.s_osc, since(2))
            with act.Fori(0, B) as b:
                act.wait_ge(k.s_conv, since(b))
                for ct in range(CT):
                    act.wait_ge(k.s_xn, since(CT * b + ct + 1))
                    act.activation(xp[:, ct, 0, 1:1 + S, 1:1 + S],
                                   xn[:, ct, :].rearrange("p (i j) -> p i j", j=S), ACT.Copy
                                   ).then_inc(k.s_xphi, 1)
                act.wait_ge(k.s_xtout, since(16 * b))
                for i, ts in enumerate(TWOS):
                    act.wait_ge(k.s_tr, since(len(TWOS) * b + i + 1))
                    act.activation(xt[:, ts, 0, :], two(psT, i, ts), ACT.Copy).then_inc(k.s_xthi, 1)
                offsets_act(act, b, psA, psB, quarters, osc[:, 1:2], bo, offs, msk, k)
            wts.split_high(act, kept.inv_of("w1"), k)

        @block.tensor
        def _(pe):
            pe.wait_ge(k.s_const, since(16 * 7))
            gn_statistics_pe(pe, kept.grp, gn, k)
            pe.wait_ge(k.s_wolo, since(2))
            with pe.Fori(0, B) as b:
                pe.wait_ge(k.s_xn, since(CT * (b + 1)))
                pe.wait_ge(k.s_xtlo, since(len(TWOS) * b))
                for t in range(NB):
                    for ct in range(CT):
                        mm = pe.transpose(psT[:, t // 2, (t % 2) * C + ct * 128:
                                              (t % 2) * C + (ct + 1) * 128],
                                          xn[:, ct, t * BP:(t + 1) * BP], kept.ident[:])
                    if t % 2 or t == NB - 1:
                        mm.then_inc(k.s_tr, 1)
                pe.wait_ge(k.s_xplo, since(CT * (b + 1)))
                pe.wait_ge(k.s_quarters, since(2 * b))
                offset_conv_pe(pe, psA, lambda kt, n, h: wo[:, h, kt * TAPS + n, :],
                               lambda kt, h: xp[:, kt, h], CT).then_inc(k.s_conv, 1)
                sum_quarters_pe(pe, b, psB, kept.sel, quarters, k)



class Plan:

    def __init__(self, pairs, kept_blocks):
        self.pairs, self.loads, self.load_of = pairs, [], []
        for u, t, r in pairs:
            if r not in self.loads[-kept_blocks:]:
                self.loads.append(r)
            self.load_of.append(max(m for m, x in enumerate(self.loads) if x == r))
        loads = range(len(self.loads))
        self.first = [self.load_of.index(m) for m in loads]
        self.last = [max(n for n, x in enumerate(self.load_of) if x == m) for m in loads]

    def of_unit(self, u):
        return [n for n, p in enumerate(self.pairs) if p[0] == u]


def earlier(b, n, slots, per_image):
    return per_image * b + max(0, n - slots + 1)


def wait_both(sp, first, second):
    for _, count in (first, second):
        if not isinstance(count, int):
            sp.to_reg(since(count))
    sp.wait_ge(first[0], since(first[1]))
    sp.wait_ge(second[0], since(second[1]))


class Sampler:

    def __init__(self, nc, c, stage, kept, plan, pos_slots, g_at, g_free):
        def sb(name, shape, dt=F32):
            return c.enter_context(nc.sbuf_tensor(f"{stage}_{name}", shape, dt))
        self.kept, self.plan, self.slots = kept, plan, pos_slots
        self.row = sb("row", [BP, pos_slots, JW])
        self.cm = sb("cm", [BP, 2, 2, JW])
        self.dcol = sb("dcol", [BP, JW])
        self.col = sb("col", [BP, pos_slots, JW])
        self.drow = sb("drow", [BP, 2, JW])
        self.g = sb("g", [BP, 3, JW])
        self.g_at, self.g_free = g_at, g_free
        class Sem:
            (s_dcol, s_hcol, s_col, s_drow, s_g, s_ghi, s_glo) = semaphores(
                nc, stage,
                "dcol hcol col drow g ghi glo")
        self.k = Sem
        self.s_rowin = [semaphore(nc, f"{stage}_rowin{i}") for i in range(pos_slots)]
        self.s_cmin = [semaphore(nc, f"{stage}_cmin{i}") for i in range(2)]
        self.acts, self.dves = 0, 0

    def load(self, sp, b, n, pos_d):
        k, p = self.k, self.plan
        L, P, slot = len(p.loads), len(p.pairs), n % self.slots
        rows_used = P * b + (p.last[n - self.slots] + 1 if n >= self.slots else 0)
        wait_both(sp, (k.s_col, earlier(b, n, 2, L)), (k.s_drow, rows_used))
        src = pos_d[b, p.loads[n]]
        sp.dma_start(self.cm[:, n % 2].rearrange("p k j -> p (k j)"),
                     src[JW:3 * JW].partition_broadcast(BP)).then_inc(self.s_cmin[n % 2], 16)
        sp.dma_start(self.row[:, slot, :], src[0:JW].partition_broadcast(BP)
                     ).then_inc(self.s_rowin[slot], 16)

    def landed(self, eng, sems, b, m):
        L, slots = len(self.plan.loads), len(sems)
        in_slot = len(range(m % slots, L, slots))
        eng.wait_ge(sems[m % slots], since(16 * (in_slot * b + m // slots + 1)))

    def act(self, act, b, upto):
        k, p, negq = self.k, self.plan, self.kept.negq
        L, P = len(p.loads), len(p.pairs)
        start, upto = self.acts, min(upto, P)
        for n in range(start, upto):
            t, m = p.pairs[n][1], p.load_of[n]
            if p.first[m] == n:
                self.landed(act, self.s_cmin, b, m)
                act.wait_ge(k.s_col, since(L * b + m))
                act.activation(self.dcol[:], self.cm[:, m % 2, 0, :], ACT.Abs,
                               bias=negq[:, NB:NB + 1]).then_inc(k.s_dcol, 1)
                self.landed(act, self.s_rowin, b, m)
            act.wait_ge(k.s_g, since(P * b + max(0, n - 1)))
            act.activation(self.drow[:, n % 2, :], self.row[:, m % self.slots, :], ACT.Abs,
                           bias=negq[:, t:t + 1]).then_inc(k.s_drow, 1)
            if n > start:
                self.clamp(act, b, n - 1)
        if upto > start:
            self.clamp(act, b, upto - 1)
            self.acts = upto

    def clamp(self, act, b, n):
        k, P = self.k, len(self.plan.pairs)
        self.g_free(act, b, n)
        act.wait_ge(k.s_g, since(P * b + n + 1))
        out, shape = self.g_at(n, 0)
        act.activation(out, shape(self.g[:, n % 3, :]), ACT.Relu).then_inc(k.s_ghi, 1)

    def dve(self, dve, b, upto):
        k, p = self.k, self.plan
        L, P = len(p.loads), len(p.pairs)
        start, upto = self.dves, min(upto, P)
        for n in range(start, upto):
            t, m = p.pairs[n][1], p.load_of[n]
            if p.first[m] == n:
                dve.wait_ge(k.s_dcol, since(L * b + m + 1))
                dve.tensor_scalar(self.dcol[:], self.dcol[:], 1.0, 1.0, ALU.min, ALU.subtract
                                  ).then_inc(k.s_hcol, 1)
                dve.wait_ge(k.s_hcol, since(L * b + m + 1))
                dve.tensor_tensor(self.col[:, m % self.slots, :], self.dcol[:],
                                  self.cm[:, m % 2, 1, :], ALU.mult).then_inc(k.s_col, 1)
            dve.wait_ge(k.s_drow, since(P * b + n + 1))
            dve.wait_ge(k.s_col, since(L * b + m + 1))
            dve.wait_ge(k.s_glo, since(P * b + max(0, n - 2)))
            dve.scalar_tensor_tensor(self.g[:, n % 3, :], self.drow[:, n % 2, :], 1.0,
                                     self.col[:, m % self.slots, :], ALU.subtract, ALU.mult
                                     ).then_inc(k.s_g, 1)
            if n > start:
                self.low(dve, b, n - 1)
        if upto > start:
            self.low(dve, b, upto - 1)
            self.dves = upto

    def low(self, dve, b, n):
        k, P = self.k, len(self.plan.pairs)
        dve.wait_ge(k.s_ghi, since(P * b + n + 1))
        (hi, shape), (lo, _) = self.g_at(n, 0), self.g_at(n, 1)
        dve.scalar_tensor_tensor(lo, shape(self.g[:, n % 3, :]), 0.0, hi, ALU.max, ALU.subtract
                                 ).then_inc(k.s_glo, 1)


def neighbours(r, band):
    return [x for x in range(NB) if abs(x - r) <= band]


NEAR, ANY = 1, NB


def both_bands(eng, kept, flag, emit):
    far = eng.value_load(kept.far[0:1, flag:flag + 1], min_val=0, max_val=1)
    with eng.If(far < 1):
        emit(NEAR)
    with eng.If(far > 0):
        emit(ANY)



def stage_layer1(nc, kept, wts, xT_d, pos_d, h_d):
    with ExitStack() as c:
        def sb(name, shape, dt=F32):
            return c.enter_context(nc.sbuf_tensor("l_" + name, shape, dt))

        def psum(name, shape, dt=F32):
            return c.enter_context(nc.psum_tensor("l_" + name, shape, dt))

        GS = 4
        xt = sb("xt", [BP, NB, 2, C], F16)
        g = sb("gh", [BP, GS, 2, JW], F16)
        xo = sb("xo", [128, CT, 2, RB, JW], F16)
        hb = sb("h", [128, RB, HT, BP])
        peak = sb("peak", [128, 2])
        ps_x = psum("ps_x", [128, 2 * CT, 512])
        ps_h = psum("ps_h", [128, 4, 512])
        class Sem:
            (s_xtin, s_pair, s_xo, s_xohi, s_xolo, s_conv, s_h, s_hout, s_peak, s_hmax, s_zero) = semaphores(
                nc, "l",
                "xtin pair xo xohi xolo conv h hout peak hmax zero")
        k = Sem
        g_at = lambda n, h: (g[:, n % GS, h, :], lambda v: v)
        plans = {band: Plan([(r, t, r) for r in range(NB) for t in neighbours(r, band)], 1)
                 for band in (NEAR, ANY)}
        smp = Sampler(nc, c, "l", kept, None, 2, g_at, None)
        smp.g_free = lambda act, b, n: act.wait_ge(k.s_pair, since(earlier(b, n, GS, len(smp.plan.pairs))))
        block = stage_block(nc, c)

        def start(band):
            smp.plan, smp.acts, smp.dves = plans[band], 0, 0

        def half(h):
            return slice(h * (JW // 2), (h + 1) * (JW // 2))

        def sample_block(pe, b, plan, r):
            pairs = plan.of_unit(r)
            for n in pairs:
                pe.wait_ge(smp.k.s_glo, since(len(plan.pairs) * b + n + 1))
                t = plan.pairs[n][1]
                for ct in range(CT):
                    for h in range(2):
                        if n == pairs[0]:
                            pe.wait_ge(k.s_xolo, since(4 * NB * b + max(0, 4 * (r - 1) + 2 * ct + h + 1)))
                        mm = three_passes(pe, ps_x[:, 2 * ct + h, 0:JW // 2],
                                          lambda a: xt[:, t, a, ct * 128:(ct + 1) * 128],
                                          lambda a: g[:, n % GS, a, half(h)],
                                          n == pairs[0], n == pairs[-1])
                        if n == pairs[-1] and 2 * ct + h < 3:
                            mm.then_inc(k.s_xo, 1)
                mm.then_inc(k.s_pair, 1)

        @block.sync
        def _(sp):
            def store_h(b, i):
                sp.wait_ge(k.s_h, since(HT * (2 * b + i + 1)))
                for j, r in enumerate(GROUPS[i]):
                    sp.dma_start(h_d[b, r], hb[:, j].rearrange("p m q -> p (m q)")
                                 ).then_inc(k.s_hout, 16)

            def begin(b):
                sp.wait_ge(k.s_pair, since(len(smp.plan.pairs) * b))
                sp.dma_start(xt[:].rearrange("p t h c -> p (t h c)"), xT_d[b]).then_inc(k.s_xtin, 16)
                for r in range(2):
                    smp.load(sp, b, r, pos_d)

            def rest(b):
                for r in range(2, NB):
                    smp.load(sp, b, r, pos_d)
                store_h(b, 0)

            def emit(band):
                start(band)
                begin(0)
                rest(0)
                with sp.Fori(1, B) as b:
                    begin(b)
                    store_h(b - 1, 1)
                    rest(b)
                store_h(B - 1, 1)
                sp.wait_ge(k.s_hout, since(16 * NB * B))
            both_bands(sp, kept, 0, emit)

        @block.scalar
        def _(act):
            def emit(band):
                start(band)
                plan = smp.plan
                smp.act(act, 0, GS)

                def image(b, last):
                    for i, rs in enumerate(GROUPS):
                        for j, r in enumerate(rs):
                            smp.act(act, b, plan.last[r] + 1)
                            smp.act(act, b, plan.last[r] + GS)
                            act.wait_ge(k.s_conv, since(HT * (2 * b + i)))
                            for ct in range(CT):
                                for h in range(2):
                                    q = 2 * ct + h
                                    if q < 3:
                                        act.wait_ge(k.s_xo, since(3 * (NB * b + r) + q + 1))
                                    else:
                                        act.wait_ge(k.s_pair, since(len(plan.pairs) * b + plan.last[r] + 1))
                                    act.activation(xo[:, ct, 0, j, half(h)],
                                                   ps_x[:, 2 * ct + h, 0:JW // 2], ACT.Copy
                                                   ).then_inc(k.s_xohi, 1)
                        if not i:
                            smp.act(act, b, plan.last[rs[-1]] + GS + 1)
                        if i and not last:
                            smp.acts = 0
                            smp.act(act, b + 1, GS)
                        act.wait_ge(k.s_hout, since(16 * (NB * b + (RB if i else 0))))
                        act.wait_ge(k.s_peak, since(2 * b + i))
                        for m in range(HT):
                            act.wait_ge(k.s_conv, since(HT * (2 * b + i) + m + 1))
                            act.activation(hb[:, 0:len(rs), m, :],
                                           ps_h[:, m % 4, 0:len(rs) * BP]
                                           .rearrange("p (r q) -> p r q", q=BP), ACT.Relu,
                                           scale=kept.scale_of("w1")).then_inc(k.s_h, 1)

                with act.Fori(0, B - 1) as b:
                    image(b, False)
                image(B - 1, True)
            both_bands(act, kept, 0, emit)

        @block.vector
        def _(dve):
            dve.memset(kept.hmax[:], 0.0).then_inc(k.s_zero, 1)
            dve.wait_ge(k.s_zero, since(1))

            def emit(band):
                start(band)
                plan = smp.plan
                smp.dve(dve, 0, GS)

                def image(b, last):
                    for i, rs in enumerate(GROUPS):
                        for j, r in enumerate(rs):
                            smp.dve(dve, b, plan.last[r] + 1)
                            smp.dve(dve, b, plan.last[r] + GS)
                            for ct in range(CT):
                                for h in range(2):
                                    q = 4 * (NB * b + r) + 2 * ct + h
                                    dve.wait_ge(k.s_xohi, since(q + 1))
                                    dve.tensor_tensor(xo[:, ct, 1, j, half(h)],
                                                      ps_x[:, 2 * ct + h, 0:JW // 2],
                                                      xo[:, ct, 0, j, half(h)], ALU.subtract
                                                      ).then_inc(k.s_xolo, 1)
                        if not i:
                            smp.dve(dve, b, plan.last[rs[-1]] + GS + 1)
                        if i and not last:
                            smp.dves = 0
                            smp.dve(dve, b + 1, GS)
                        dve.wait_ge(k.s_h, since(HT * (2 * b + i + 1)))
                        dve.tensor_reduce(peak[:, 0:1], hb[:, 0:len(rs)], AX.XYZ, ALU.max
                                          ).then_inc(k.s_peak, 1)
                        dve.wait_ge(k.s_peak, since(2 * b + i + 1))
                        dve.tensor_tensor(kept.hmax[:, 0:1], kept.hmax[:, 0:1], peak[:, 0:1],
                                          ALU.max).then_inc(k.s_hmax, 1)
                        dve.wait_ge(k.s_hmax, since(2 * b + i + 1))

                with dve.Fori(0, B - 1) as b:
                    image(b, False)
                image(B - 1, True)
            both_bands(dve, kept, 0, emit)

        @block.tensor
        def _(pe):
            def emit(band):
                start(band)
                plan = smp.plan
                with pe.Fori(0, B) as b:
                    pe.wait_ge(k.s_xtin, since(16 * (b + 1)))
                    for i, rs in enumerate(GROUPS):
                        for r in rs:
                            sample_block(pe, b, plan, r)
                        pe.wait_ge(k.s_xolo, since(4 * (NB * b + rs[-1] + 1)))
                        for m in range(HT):
                            pe.wait_ge(k.s_h, since(earlier(2 * b + i, m, 4, HT)))
                            for kt in range(CT * TAPS):
                                ct, n = divmod(kt, TAPS)
                                mm = three_passes(
                                    pe, ps_h[:, m % 4, 0:len(rs) * BP],
                                    lambda a: wts.half(kt, a)[:, m * 128:(m + 1) * 128],
                                    lambda a: xo[:, ct, a, 0:len(rs), n * BP:(n + 1) * BP],
                                    kt == 0, kt == CT * TAPS - 1)
                            mm.then_inc(k.s_conv, 1)
            both_bands(pe, kept, 0, emit)



def stage_offsets2(nc, kept, wts, w2, woff2, boff2, consts, h_d, pos_d):
    with ExitStack() as c:
        def sb(name, shape, dt=F32):
            return c.enter_context(nc.sbuf_tensor("o_" + name, shape, dt))

        def psum(name, shape, dt=F32):
            return c.enter_context(nc.psum_tensor("o_" + name, shape, dt))

        HS = 3
        hs = sb("h", [128, HS, HT, BP])
        hp = sb("hp", [128, 2, HT, 2, PADW, PADW], F16)
        wo32 = sb("wo32", [128, HT * TAPS, OFF])
        wo = sb("wo", [128, 2, HT * TAPS, 32], F16)
        maxes, most = sb("maxes", [128, W_SLOTS + 1]), sb("most", [128, 1])
        maxes2, most2 = sb("maxes2", [128, 2]), sb("most2", [128, 2])
        bo, osc = sb("bo", [OFF, 1]), sb("osc", [OFF, 2])
        p0n = sb("p0n", [OFF, PIX])
        quarters = sb("quarters", [128, 2, HALF])
        offs, pos, msk = (sb(n, [OFF, 2, HALF]) for n in ("offs", "pos", "msk"))
        reach = sb("reach", [128, B + 2])
        psA, psB = psum("psA", [128, 2, 512]), psum("psB", [128, 2, 512])
        class Sem:
            (s_const, s_wo, s_w, s_womax, s_woscale, s_wohi, s_wolo, s_osc, s_wmax, s_wscale, s_whi,
             s_wlo, s_hall, s_hscale, s_zero, s_hphi, s_hplo, s_conv, s_quarters, s_sum,
             s_pos, s_msk, s_offs, s_reach, s_posout, s_far) = semaphores(
                nc, "o",
                "const wo w womax woscale wohi wolo osc wmax wscale whi wlo hall hscale zero "
                "hphi hplo conv quarters sum pos msk offs reach posout far")
        k = Sem
        s_hin = [semaphore(nc, f"o_hin{i}") for i in range(HS)]
        block = stage_block(nc, c)
        ROUND = 2 * NB
        USES = [len(range(i, ROUND, HS)) for i in range(HS)]

        PARTS = B - 2

        def by_image(eng, first, second, weights):
            first(0, 0)
            first(0, 1)
            second(0)
            with eng.Fori(1, B // 2) as bb:
                first(bb, 0)
                second(2 * bb - 1)
                first(bb, 1)
                second(2 * bb)
            weights()
            second(B - 1)

        def inner(half, i, t):
            return hp[:, i, :, half, 1 + RB * t:1 + RB * (t + 1), 1:1 + S]

        def as_words(image):
            return image.rearrange("p m h i j -> p (m h i j)").bitcast(F32)

        def as_rows(slot):
            return hs[:, slot].rearrange("p m (i j) -> p m i j", j=S)

        @block.sync
        def _(sp):
            sp.dma_start(p0n[:], consts["p0n"]).then_inc(k.s_const, 16)
            sp.dma_start(bo[:], boff2).then_inc(k.s_const, 16)
            sp.dma_start(wo32[:], woff2).then_inc(k.s_wo, 16)

            def load(bb, i):
                for n in range(NB * i, NB * (i + 1)):
                    sp.wait_ge(k.s_hplo, since(earlier(bb, n, HS, ROUND)))
                    sp.dma_start(hs[:, n % HS].rearrange("p m q -> p (m q)"),
                                 h_d[bb * 2 + i, n % NB]).then_inc(s_hin[n % HS], 16)

            def after(b):
                if isinstance(b, int) and b == 0:
                    wts.load(sp, w2, k)
                store_positions_sp(sp, b, pos_d[b], pos, msk, k)
            by_image(sp, load, after, lambda: None)
            sp.wait_ge(k.s_posout, since(32 * B))

        @block.gpsimd
        def _(pool):
            pool.memset(wo[:], 0.0).then_inc(k.s_zero, 1)
            pool.partition_all_reduce(kept.hmax[:, 1:2], kept.hmax[:, 0:1], 128, ABSMAX
                                      ).then_inc(k.s_hall, 1)
            pool.memset(reach[:], 0.0).then_inc(k.s_zero, 1)
            offset_weights_pool(pool, maxes2, most2, k)
            pool.memset(as_words(hp[:, 0]), 0.0).then_inc(k.s_zero, 1)
            largest_weight_pool(pool, maxes, most, k, PARTS)
            far_flag_pool(pool, reach, k)

        @block.vector
        def _(dve):
            dve.memset(as_words(hp[:, 1]), 0.0).then_inc(k.s_zero, 1)
            dve.wait_ge(k.s_hall, since(1))
            power_of_two(dve, k.s_hscale, kept.hmax[:, 1:2], kept.scale_of("h"), kept.inv_of("h"))
            dve.wait_ge(k.s_const, since(16 * 2))
            offset_weights_dve(dve, wo32, wo, maxes2, most2, osc, kept, k, "p2", "m2",
                               kept.scale_of("h", OFF))
            dve.wait_ge(k.s_zero, since(4))

            def split(bb, i):
                for t in range(NB):
                    n = NB * i + t
                    dve.wait_ge(k.s_hphi, since(ROUND * bb + n + 1))
                    for m in range(HT):
                        ins = dve.scalar_tensor_tensor(
                            inner(1, i, t)[:, m], as_rows(n % HS)[:, m], kept.inv_of("h"),
                            inner(0, i, t)[:, m], ALU.mult, ALU.subtract)
                    ins.then_inc(k.s_hplo, 1)

            def after(b):
                if not isinstance(b, int):
                    wts.largest(dve, maxes, k, b - 1, PARTS)
                positions_dve(dve, b, offs, p0n, pos, reach, k)

            def weights():
                wts.largest_of_parts(dve, maxes, k, PARTS)
                dve.wait_ge(k.s_wmax, since(PARTS + 2))
                power_of_two(dve, k.s_wscale, most[:], kept.scale_of("w2"), kept.inv_of("w2"))
                wts.split_low(dve, kept.inv_of("w2"), k)
            by_image(dve, split, after, weights)
            far_flag_dve(dve, reach, kept.rows, kept.far[:, 1:2], k)

        @block.scalar
        def _(act):
            offset_weights_act(act, wo32, wo, kept, k, "p2", "m2")
            act.wait_ge(k.s_zero, since(4))
            act.wait_ge(k.s_hscale, since(3))
            act.wait_ge(k.s_const, since(16 * 2))
            act.wait_ge(k.s_osc, since(3))

            def split(bb, i):
                if not (isinstance(bb, int) and bb == 0):
                    act.wait_ge(k.s_conv, since(2 * bb + i - 1))
                for t in range(NB):
                    n = NB * i + t
                    act.wait_ge(s_hin[n % HS], since(16 * (USES[n % HS] * bb + n // HS + 1)))
                    for m in range(HT):
                        ins = act.activation(inner(0, i, t)[:, m], as_rows(n % HS)[:, m], ACT.Copy,
                                             scale=kept.inv_of("h"))
                    ins.then_inc(k.s_hphi, 1)
            by_image(act, split, lambda b: offsets_act(act, b, psA, psB, quarters, osc[:, 1:2], bo,
                                                       offs, msk, k),
                     lambda: wts.split_high(act, kept.inv_of("w2"), k))

        @block.tensor
        def _(pe):
            pe.wait_ge(k.s_wolo, since(2))
            with pe.Fori(0, B // 2) as bb:
                for i in range(2):
                    b = 2 * bb + i
                    pe.wait_ge(k.s_hplo, since(NB * (b + 1)))
                    pe.wait_ge(k.s_quarters, since(2 * b))
                    offset_conv_pe(pe, psA, lambda kt, n, h: wo[:, h, kt * TAPS + n, :],
                                   lambda kt, h: hp[:, i, kt, h], HT).then_inc(k.s_conv, 1)
                    sum_quarters_pe(pe, b, psB, kept.sel, quarters, k)



def stage_layer2(nc, kept, wts, h_d, pos_d, x, x1_d):
    with ExitStack() as c:
        def sb(name, shape, dt=F32):
            return c.enter_context(nc.sbuf_tensor("m_" + name, shape, dt))

        def psum(name, shape, dt=F32):
            return c.enter_context(nc.psum_tensor("m_" + name, shape, dt))

        WIDE = 3 * BP
        YC = [(2 * j, min(2, TAPS - 2 * j)) for j in range(5)]
        NY = len(YC)
        YS = 4
        hs = sb("h", [128, 2, HT * BP])
        hh = sb("hh", [128, 2, 2, HT, BP], F16)
        g = sb("gh", [BP, 2, 2, TAPS, WIDE], F16)
        ys = sb("y", [BP, YS, 2, 2 * C], F16)
        xr = sb("xr", [128, CT, PIX])
        sw = sb("sw", [128, 1])
        ps_y = psum("ps_y", [BP, YS, 512])
        ps_o = psum("ps_o", [128, 2 * CT, 512])
        class Sem:
            (s_hhhi, s_hhlo, s_y, s_yhi, s_ylo, s_unit, s_out, s_fin, s_xin, s_xout, s_sw,
             s_stats) = semaphores(
                nc, "m",
                "hhhi hhlo y yhi ylo unit out fin xin xout sw stats")
        k = Sem
        s_hin = [semaphore(nc, f"m_hin{i}") for i in range(2)]

        def units(band):
            if band == NEAR:
                return [(t, neighbours(t, NEAR)) for t in range(NB)]
            return [(t, list(range(a, min(a + 3, NB)))) for t in range(NB) for a in range(0, NB, 3)]

        UN = {band: units(band) for band in (NEAR, ANY)}
        plans = {band: Plan([(u, t, r) for u, (t, rs) in enumerate(UN[band]) for r in rs],
                            3 if band == NEAR else 1) for band in (NEAR, ANY)}
        now = {}

        def g_at(n, h):
            u, _, r = smp.plan.pairs[n]
            at = (r - now["units"][u][1][0]) * BP
            return g[:, u % 2, h, :, at:at + BP], lambda v: v.rearrange("p (k q) -> p k q", q=BP)

        def g_free(act, b, n):
            u = smp.plan.pairs[n][0]
            act.wait_ge(k.s_unit, since(earlier(b, u, 2, len(now["units"]))))

        smp = Sampler(nc, c, "m", kept, None, 4, g_at, g_free)
        block = stage_block(nc, c)

        def start(band):
            smp.plan, smp.acts, smp.dves = plans[band], 0, 0
            now["units"] = UN[band]

        def pieces(u):
            rs = now["units"][u][1]
            for i, grp in enumerate(GROUPS):
                both = [r for r in rs if r in grp]
                if both:
                    a, w = (both[0] - rs[0]) * BP, len(both) * BP
                    at = (both[0] - grp[0]) * BP
                    yield i, slice(a, a + w), slice(at, at + w)

        @block.sync
        def _(sp):
            def store(b):
                sp.wait_ge(k.s_fin, since(2 * CT * (b + 1)))
                sp.dma_start(x1_d[b], xr[:].rearrange("p k q -> p (k q)")).then_inc(k.s_xout, 16)

            def emit(band):
                start(band)
                U = len(now["units"])

                def image(b, first):
                    done = 0
                    for u in range(U):
                        sp.wait_ge(k.s_hhlo, since(earlier(b, u, 2, U)))
                        sp.dma_start(hs[:, u % 2], h_d[b, now["units"][u][0]]
                                     ).then_inc(s_hin[u % 2], 16)
                        need = smp.plan.load_of[smp.plan.of_unit(u)[-1]] + 1
                        for m in range(done, need):
                            smp.load(sp, b, m, pos_d)
                        done = need
                        if u == 2:
                            if not first:
                                store(b - 1)
                            wait_both(sp, (k.s_xout, 16 * b), (k.s_stats, 2 * CT * b))
                            sp.dma_start(xr[:], x[b].rearrange("(k p) i j -> p k (i j)", p=128)
                                         ).then_inc(k.s_xin, 16)

                image(0, True)
                with sp.Fori(1, B) as b:
                    image(b, False)
                store(B - 1)
                sp.wait_ge(k.s_xout, since(16 * B))
            both_bands(sp, kept, 1, emit)

        def hin(eng, b, u, U):
            eng.wait_ge(s_hin[u % 2], since(16 * (len(range(u % 2, U, 2)) * b + u // 2 + 1)))

        def used(eng, b, y, U):
            n = y - YS
            if n < 0:
                eng.wait_ge(k.s_unit, since(U * b))
            elif n % NY == NY - 1:
                eng.wait_ge(k.s_unit, since(U * b + n // NY + 1))
            else:
                eng.wait_ge(k.s_out, since((NY - 1) * (U * b + n // NY) + n % NY + 1))

        @block.scalar
        def _(act):
            def emit(band):
                start(band)
                U = len(now["units"])

                def split(b, u):
                    hin(act, b, u, U)
                    act.wait_ge(k.s_y, since(NY * earlier(b, u, 2, U)))
                    act.activation(hh[:, u % 2, 0].rearrange("p m q -> p (m q)"), hs[:, u % 2],
                                   ACT.Copy, scale=kept.inv_of("h")).then_inc(k.s_hhhi, 1)

                with act.Fori(0, B) as b:
                    split(b, 0)
                    smp.act(act, b, smp.plan.of_unit(0)[-1] + 1)
                    for u in range(U):
                        ahead = smp.plan.of_unit(u + 1) if u + 1 < U else []
                        for j, (n0, nt) in enumerate(YC):
                            y = NY * u + j
                            act.wait_ge(k.s_y, since(NY * U * b + y + 1))
                            used(act, b, y, U)
                            act.activation(ys[:, y % YS, 0, 0:nt * C], ps_y[:, y % YS, 0:nt * C],
                                           ACT.Copy).then_inc(k.s_yhi, 1)
                            if ahead and j == 1:
                                split(b, u + 1)
                            if ahead and 1 <= j <= len(ahead):
                                smp.act(act, b, ahead[j - 1] + 1)
                    smp.acts = 0
            both_bands(act, kept, 1, emit)

        @block.vector
        def _(dve):
            dve.tensor_tensor(sw[:], kept.scale_of("w2"), kept.scale_of("h"), ALU.mult
                              ).then_inc(k.s_sw, 1)
            dve.wait_ge(k.s_sw, since(1))

            def emit(band):
                start(band)
                U = len(now["units"])

                def split(b, u):
                    dve.wait_ge(k.s_hhhi, since(U * b + u + 1))
                    dve.scalar_tensor_tensor(hh[:, u % 2, 1].rearrange("p m q -> p (m q)"),
                                             hs[:, u % 2], kept.inv_of("h"),
                                             hh[:, u % 2, 0].rearrange("p m q -> p (m q)"),
                                             ALU.mult, ALU.subtract).then_inc(k.s_hhlo, 1)

                def statistics(b):
                    dve.wait_ge(k.s_fin, since(2 * CT * (b + 1)))
                    for mt in range(CT):
                        for h in range(2):
                            dve.bn_stats(kept.stats[:, bass.ds(b * CT + mt, 1), h, :]
                                         .rearrange("p b s -> p (b s)"),
                                         xr[:, mt, h * HALF:(h + 1) * HALF]).then_inc(k.s_stats, 1)

                def image(b, first, last):
                    smp.dve(dve, b, smp.plan.of_unit(0)[-1] + 1)
                    for u in range(U):
                        if u == 1 and not first:
                            statistics(b - 1)
                        ahead = smp.plan.of_unit(u + 1) if u + 1 < U else []
                        for j, (n0, nt) in enumerate(YC):
                            y = NY * u + j
                            dve.wait_ge(k.s_yhi, since(NY * U * b + y + 1))
                            dve.tensor_tensor(ys[:, y % YS, 1, 0:nt * C], ps_y[:, y % YS, 0:nt * C],
                                              ys[:, y % YS, 0, 0:nt * C], ALU.subtract
                                              ).then_inc(k.s_ylo, 1)
                            if ahead and j == 1:
                                split(b, u + 1)
                            if ahead and 1 <= j <= len(ahead):
                                smp.dve(dve, b, ahead[j - 1] + 1)
                    smp.dves = 0
                    if not last:
                        split(b + 1, 0)
                    dve.wait_ge(k.s_unit, since(U * (b + 1)))
                    dve.wait_ge(k.s_xin, since(16 * (b + 1)))
                    for mt in range(CT):
                        for i, grp in enumerate(GROUPS):
                            w = len(grp) * BP
                            into = xr[:, mt, grp[0] * BP:grp[0] * BP + w]
                            dve.scalar_tensor_tensor(into, ps_o[:, 2 * mt + i, 0:w], sw[:, 0:1],
                                                     into, ALU.mult, ALU.add).then_inc(k.s_fin, 1)

                split(0, 0)
                image(0, True, False)
                with dve.Fori(1, B - 1) as b:
                    image(b, False, False)
                image(B - 1, False, True)
                statistics(B - 1)
            both_bands(dve, kept, 1, emit)

        @block.tensor
        def _(pe):
            def emit(band):
                start(band)
                U = len(now["units"])

                def products(b, u, j):
                    n0, nt = YC[j]
                    y = NY * u + j
                    if j == 0:
                        pe.wait_ge(k.s_hhlo, since(U * b + u + 1))
                    pe.wait_ge(k.s_ylo, since(earlier(b, y, YS, NY * U)))
                    for m in range(HT):
                        at = 4096 * j + m * nt * C
                        mm = three_passes(pe, ps_y[:, y % YS, 0:nt * C],
                                          lambda a: hh[:, u % 2, a, m, :],
                                          lambda a: wts.half(at // W_SLOT, a)
                                          [:, at % W_SLOT:at % W_SLOT + nt * C],
                                          m == 0, m == HT - 1)
                    mm.then_inc(k.s_y, 1)

                def sample(b, u, j, begun):
                    n0, nt = YC[j]
                    y = NY * u + j
                    if j == 0:
                        pe.wait_ge(smp.k.s_glo, since(len(smp.plan.pairs) * b
                                   + smp.plan.of_unit(u)[-1] + 1))
                    if u == 0 and j == 0:
                        pe.wait_ge(k.s_fin, since(2 * CT * b))
                    pe.wait_ge(k.s_ylo, since(NY * U * b + y + 1))
                    for d in range(nt):
                        for mt in range(CT):
                            for i, cols, at in pieces(u):
                                first = (mt, i) not in begun
                                begun.add((mt, i))
                                mm = three_passes(
                                    pe, ps_o[:, 2 * mt + i, at],
                                    lambda a: ys[:, y % YS, a, d * C + mt * 128:
                                                 d * C + (mt + 1) * 128],
                                    lambda a: g[:, u % 2, a, n0 + d, cols], first, True)
                    mm.then_inc(k.s_unit if j == NY - 1 else k.s_out, 1)

                with pe.Fori(0, B) as b:
                    begun = set()
                    steps = [(u, j) for u in range(U) for j in range(NY)]
                    products(b, 0, 0)
                    for n, (u, j) in enumerate(steps):
                        if n + 1 < len(steps):
                            products(b, *steps[n + 1])
                        sample(b, u, j, begun)
            both_bands(pe, kept, 1, emit)



def stage_attention(nc, kept, ins, x1_d, qk_d, out):
    with ExitStack() as c:
        def sb(name, shape, dt=F32):
            return c.enter_context(nc.sbuf_tensor("a_" + name, shape, dt))

        def psum(name, shape, dt=F32):
            return c.enter_context(nc.psum_tensor("a_" + name, shape, dt))

        NW, KT = len(WINDOWS), len(WINDOWS) * CT
        CW = NW * VW
        reaches = [window_blocks(S // w) for w in WINDOWS]

        def reached(w, t):
            return [r for r in range(NB) if reaches[w][0] <= r - t <= reaches[w][1]]

        wide = [max(len(reached(w, t)) for t in range(NB)) * BP for w in range(NW)]
        xb = sb("x", [128, 2, CT, PIX])
        xn = sb("xn", [128, CT, PIX])
        xh = sb("xh", [128, CT, 2, PIX], F16)
        gn = gn_buffers(sb, kept.stats)
        cur = sb("cur", [128, 2 * CT])
        wqkv = sb("wqkv", [128, 2, CT, 3, C], F16)
        wo = sb("wo", [128, 2, KT, C], F16)
        maxes, most = sb("maxes", [128, 4]), sb("most", [128, 4])
        so = sb("so", [128, 1])
        bo = sb("bo", [128, CT])
        qf = sb("qf", [128, 2, PIX])
        qh = sb("qh", [128, 2 * CT, 2, PIX], F16)
        stacks = sb("stacks", [96, 2, HEADS, PIX], F16)
        vf = sb("vf", [BP, NB, C])
        norm = sb("norm", [BP, 2, NB * HEADS])
        v = sb("v", [BP, NB, HEADS, VW], F16)
        SS = 3
        sh = sb("sh", [BP, SS, 2, PIX], F16)
        sm = [sb(f"sm{w}", [BP, SS, 2, wide[w]], F16) for w in range(NW)]
        POOLS = 1
        masks = sb("masks", [BP, NW, (2 * NB - 1) * BP], F16)
        av = sb("av", [BP, NB * NW, VW])
        rec = sb("rec", [BP, 2, NB * NW])
        num = sb("num", [BP, NB * NW, HD])
        o = sb("o", [128, NB * NW, C])
        ot = sb("ot", [128, KT, 2, PIX], F16)
        sq = sm[0][:].rearrange("p s h q -> p (s h q)").bitcast(F32)[:, 0:NB * C]
        w32 = o[:].rearrange("p a b -> p (a b)")
        w32qkv = w32[:, 0:CT * 3 * C].rearrange("p (t i o) -> p t i o", t=CT, i=3)
        w32o = w32[:, CT * 3 * C:CT * 3 * C + KT * C].rearrange("p (t o) -> p t o", t=KT)
        ps_s = psum("ps_s", [128, 2, 2, 512])
        ps_a = psum("ps_a", [128, 4, 512])
        class Sem:
            (s_const, s_w, s_wmax, s_wscale, s_whi, s_wlo, s_gn, s_gmm, s_sqrt, s_so, s_ones, s_x, s_res,
             s_cur, s_xn, s_xhi, s_xlo, s_qk, s_sig, s_qhi, s_qlo, s_qout, s_stack, s_vps, s_vf,
             s_sq, s_n2, s_n1, s_rn, s_vn, s_vhi, s_vlo, s_s, s_shi, s_slo, s_sm, s_smp, s_avt, s_av,
             s_avs, s_den, s_rec, s_num, s_o, s_tr, s_othi, s_otlo, s_y, s_ysum, s_ybias, s_yout) = semaphores(
                nc, "a",
                "const w wmax wscale whi wlo gn gmm sqrt so ones x res cur xn xhi xlo qk sig qhi qlo "
                "qout stack vps vf sq n2 n1 rn vn vhi vlo s shi slo sm smp avt av avs den rec num o "
                "tr othi otlo y ysum ybias yout")
        k = Sem
        gn.ps_mean, gn.ps_var = ps_a[:, 0, 0:B * CT], ps_a[:, 1, 0:B * CT]
        block = stage_block(nc, c)
        BANKS = (NB + 1) // 2
        NS = HEADS * NB

        def halves(ps):
            return ps[:, :, 0:HALF]

        def flat_s(n):
            return ps_s[0:BP, n % 2].rearrange("p h q -> p (h q)")

        def columns(w, t):
            rs = reached(w, t)
            return rs[0] * BP, (rs[-1] + 1) * BP

        def in_two(t):
            return t.rearrange("p (h q) -> p h q", q=HALF)

        @block.sync
        def _(sp):
            sp.dma_start(w32qkv, ins["wqkv"]).then_inc(k.s_w, 16)
            sp.dma_start(w32o, ins["wout"]).then_inc(k.s_w, 16)

            def load(b):
                if not (isinstance(b, int) and b == 0):
                    wait_both(sp, (k.s_res, b), (k.s_xn, CT * b))
                sp.dma_start(xb[:, 0].rearrange("p k q -> p (k q)"), x1_d[b]).then_inc(k.s_x, 16)

            def stack(b):
                for i in range(2):
                    wait_both(sp, (k.s_stack, 192 * b), (k.s_qlo, 2 * CT * b + CT * (i + 1)))
                    sp.dma_start(qk_d[i].rearrange("m p h q -> p m h q"),
                                 qh[:, CT * i:CT * (i + 1)]).then_inc(k.s_qout, 16)
                wait_both(sp, (k.s_qout, 32 * (b + 1)), (k.s_s, NS * b))
                for i, order in enumerate(((0, 0, 1), (0, 1, 0))):
                    for j, h in enumerate(order):
                        for m in range(CT):
                            src = qk_d[i, m].rearrange("(a d) h q -> d a h q", d=HD)[:, :, h, :]
                            sp.dma_start(stacks[HD * j:HD * (j + 1), i, m * 4:(m + 1) * 4, :], src
                                         ).then_inc(k.s_stack, 16)

            def store(b):
                sp.wait_ge(k.s_ybias, since(CT * (b + 1)))
                sp.dma_start(out[b].rearrange("(k p) i j -> p k (i j)", p=128), xb[:, 1]
                             ).then_inc(k.s_yout, 16)
            load(0)
            sp.dma_start(bo[:], ins["bout"]).then_inc(k.s_const, 16)
            sp.dma_start(masks[:], ins["masks"]).then_inc(k.s_const, 16)
            stack(0)
            with sp.Fori(0, B - 1) as b:
                load(b + 1)
                stack(b + 1)
                store(b)
            store(B - 1)
            sp.wait_ge(k.s_yout, since(16 * B))

        def used_masked(eng, b, n):
            m = n - SS
            if m < 0:
                eng.wait_ge(k.s_av, since(HEADS * b))
            elif m % NB == NB - 1:
                eng.wait_ge(k.s_av, since(HEADS * b + m // NB + 1))
            else:
                eng.wait_ge(k.s_avt, since((NB - 1) * (HEADS * b + m // NB) + m % NB + 1))

        def mask(eng, n, w):
            t = n % NB
            a, z = columns(w, t)
            m = (reached(w, t)[0] - t + NB - 1) * BP
            return eng.tensor_tensor(sm[w][:, n % SS, :, 0:z - a], sh[:, n % SS, :, a:z],
                                     masks[:, w, m:m + z - a].unsqueeze(1)
                                     .broadcast_to([BP, 2, z - a]), ALU.mult)

        @block.gpsimd
        def _(pool):
            pool.memset(v[:, :, :, HD:HD + 1], V_UP).then_inc(k.s_ones, 1)
            pool.wait_ge(k.s_wmax, since(4))
            pool.partition_all_reduce(most[:], maxes[:], 128, ABSMAX).then_inc(k.s_wmax, 1)
            pool.wait_ge(k.s_const, since(32))
            with pool.Fori(0, B) as b:
                for n in range(NS):
                    pool.wait_ge(k.s_slo, since(NS * b + n + 1))
                    used_masked(pool, b, n)
                    mask(pool, n, POOLS).then_inc(k.s_smp, 1)

        KEEP, AHEAD = NS // 5, NS // 2
        NAMES = ("q", "k", "v")

        def sums(act, b, head):
            g = HEADS * b + head
            act.wait_ge(k.s_av, since(g + 1))
            act.wait_ge(k.s_o, since(g))
            flat = av[:].rearrange("p a d -> p (a d)")
            for i in range(BANKS):
                n = min(2, NB - 2 * i) * CW
                act.activation(flat[:, 2 * i * CW:2 * i * CW + n], ps_a[0:BP, i, 0:n], ACT.Copy
                               ).then_inc(k.s_avs, 1)

        def attention(dve, b, head):
            g = HEADS * b + head
            dve.wait_ge(k.s_avs, since(BANKS * (g + 1)))
            dve.tensor_scalar(rec[:, 0, :], av[:, :, HD], NORM_EPS, None, ALU.add
                              ).then_inc(k.s_den, 1)
            dve.tensor_tensor(num[:], av[:, :, 0:HD], av[:, :, HD + 1:VW], ALU.add
                              ).then_inc(k.s_num, 1)
            dve.wait_ge(k.s_den, since(g + 1))
            dve.reciprocal(rec[:, 1, :], rec[:, 0, :]).then_inc(k.s_rec, 1)
            dve.wait_ge(k.s_rec, since(g + 1))
            dve.wait_ge(k.s_num, since(g + 1))
            dve.wait_ge(k.s_tr, since(2 * KT * b))
            dve.tensor_tensor(o[0:BP, :, head * HD:(head + 1) * HD], num[:],
                              rec[:, 1, :].unsqueeze(2).broadcast_to([BP, NB * NW, HD]),
                              ALU.mult).then_inc(k.s_o, 1)

        @block.vector
        def _(dve):
            dve.wait_ge(k.s_w, since(32))
            for i in range(3):
                dve.tensor_reduce(maxes[:, i:i + 1], w32qkv[:, :, i, :], AX.XY, ALU.max,
                                  apply_absolute_value=True).then_inc(k.s_wmax, 1)
            dve.tensor_reduce(maxes[:, 3:4], w32o, AX.XY, ALU.max, apply_absolute_value=True
                              ).then_inc(k.s_wmax, 1)
            dve.wait_ge(k.s_wmax, since(5))
            a = SCALES["q"]
            power_of_two(dve, k.s_wscale, most[:], kept.scale[:, a:a + 4], kept.inv[:, a:a + 4])
            dve.tensor_scalar(so[:], kept.scale_of("o"), 1 / O_UP, None, ALU.mult).then_inc(k.s_so, 1)
            dve.wait_ge(k.s_so, since(1))
            for i, name in enumerate(NAMES):
                dve.wait_ge(k.s_whi, since(i + 1))
                dve.scalar_tensor_tensor(wqkv[:, 1, :, i, :], w32qkv[:, :, i, :], kept.inv_of(name),
                                         wqkv[:, 0, :, i, :], ALU.mult, ALU.subtract
                                         ).then_inc(k.s_wlo, 1)
            dve.wait_ge(k.s_whi, since(4))
            dve.scalar_tensor_tensor(wo[:, 1], w32o, kept.inv_of("o"), wo[:, 0], ALU.mult,
                                     ALU.subtract).then_inc(k.s_wlo, 1)
            gn_groups_dve(dve, gn, k)
            dve.wait_ge(k.s_const, since(32))
            dve.wait_ge(k.s_wlo, since(4))

            def norm_of(b):
                dve.tensor_copy(cur[:], gn.cols[:, bass.ds(b, 1), :].rearrange("p b c -> p (b c)")
                                ).then_inc(k.s_cur, 1)
                dve.wait_ge(k.s_cur, since(b + 1))
                dve.wait_ge(k.s_x, since(16 * (b + 1)))
                for ct in range(CT):
                    dve.tensor_scalar(xn[:, ct, :], xb[:, 0, ct, :], cur[:, ct:ct + 1],
                                      cur[:, CT + ct:CT + ct + 1], ALU.subtract, ALU.mult
                                      ).then_inc(k.s_xn, 1)
                for ct in range(CT):
                    dve.wait_ge(k.s_xhi, since(CT * b + ct + 1))
                    dve.tensor_tensor(xh[:, ct, 1, :], xn[:, ct, :], xh[:, ct, 0, :], ALU.subtract
                                      ).then_inc(k.s_xlo, 1)

            def project(b):
                for i in range(2 * CT):
                    dve.wait_ge(k.s_qhi, since(2 * CT * b + i + 1))
                    dve.scalar_tensor_tensor(qh[:, i, 1, :], qf[:, i % 2, :], Q_UP, qh[:, i, 0, :],
                                             ALU.mult, ALU.subtract).then_inc(k.s_qlo, 1)

            def norm_v(b):
                dve.wait_ge(k.s_vf, since(NB * (b + 1)))
                dve.wait_ge(k.s_av, since(HEADS * b))
                flat = vf[:].rearrange("p t c -> p (t c)")
                dve.tensor_tensor(sq, flat, flat, ALU.mult).then_inc(k.s_sq, 1)
                dve.wait_ge(k.s_sq, since(b + 1))
                dve.tensor_reduce(norm[:, 0, :], sq.rearrange("p (h d) -> p h d", d=HD), AX.X,
                                  ALU.add).then_inc(k.s_n2, 1)
                dve.wait_ge(k.s_n1, since(b + 1))
                dve.tensor_scalar(norm[:, 1, :], norm[:, 1, :], 1e-12, None, ALU.max
                                  ).then_inc(k.s_rn, 1)
                dve.wait_ge(k.s_rn, since(2 * b + 1))
                dve.reciprocal(norm[:, 1, :], norm[:, 1, :]).then_inc(k.s_rn, 1)
                dve.wait_ge(k.s_rn, since(2 * b + 2))
                by_head = flat.rearrange("p (h d) -> p h d", d=HD)
                dve.tensor_tensor(by_head, by_head, norm[:, 1, :].unsqueeze(2)
                                  .broadcast_to([BP, NB * HEADS, HD]), ALU.mult).then_inc(k.s_vn, 1)
                vv = v[:].rearrange("p t h d -> p (t h) d")
                dve.wait_ge(k.s_vhi, since(b + 1))
                dve.scalar_tensor_tensor(vv[:, :, HD + 1:VW], by_head, V_UP, vv[:, :, 0:HD],
                                         ALU.mult, ALU.subtract).then_inc(k.s_vlo, 1)

            def image(b, last):
                for n in range(NS + 1):
                    if n == AHEAD and not last:
                        norm_of(b + 1)
                    if n < NS:
                        a, z = columns(0, n % NB)
                        dve.wait_ge(k.s_shi, since(NS * b + n + 1))
                        dve.scalar_tensor_tensor(sh[:, n % SS, 1, a:z], flat_s(n)[:, a:z], S_DOWN,
                                                 sh[:, n % SS, 0, a:z], ALU.mult, ALU.subtract
                                                 ).then_inc(k.s_slo, 1)
                    if n == 0:
                        continue
                    dve.wait_ge(k.s_slo, since(NS * b + n))
                    used_masked(dve, b, n - 1)
                    for w in range(NW):
                        if w != POOLS:
                            mask(dve, n - 1, w).then_inc(k.s_sm, 1)
                    head, t = divmod(n - 1, NB)
                    if t == 2 and head:
                        attention(dve, b, head - 1)
                attention(dve, b, HEADS - 1)
                if not last:
                    project(b + 1)
                for kt in range(KT):
                    for i, grp in enumerate(GROUPS):
                        n = 2 * kt + i
                        a, w = grp[0] * BP, len(grp) * BP
                        dve.wait_ge(k.s_othi, since(2 * KT * b + n + 1))
                        dve.scalar_tensor_tensor(ot[:, kt, 1, a:a + w], ps_s[:, kt % 2, i, 0:w],
                                                 O_UP, ot[:, kt, 0, a:a + w], ALU.mult,
                                                 ALU.subtract).then_inc(k.s_otlo, 1)
                if not last:
                    norm_v(b + 1)
                dve.wait_ge(k.s_res, since(b + 1))
                for mt in range(CT):
                    for i, grp in enumerate(GROUPS):
                        a, w = grp[0] * BP, len(grp) * BP
                        dve.wait_ge(k.s_y, since(2 * CT * b + 2 * mt + i + 1))
                        dve.scalar_tensor_tensor(xb[:, 1, mt, a:a + w], ps_a[:, 2 * mt + i, 0:w],
                                                 so[:, 0:1], xb[:, 1, mt, a:a + w], ALU.mult,
                                                 ALU.add).then_inc(k.s_ysum, 1)

            norm_of(0)
            project(0)
            norm_v(0)
            with dve.Fori(0, B - 1) as b:
                image(b, False)
            image(B - 1, True)

        @block.scalar
        def _(act):
            act.wait_ge(k.s_wscale, since(3))
            for i, name in enumerate(NAMES):
                act.activation(wqkv[:, 0, :, i, :], w32qkv[:, :, i, :], ACT.Copy,
                               scale=kept.inv_of(name)).then_inc(k.s_whi, 1)
            act.activation(wo[:, 0], w32o, ACT.Copy, scale=kept.inv_of("o")).then_inc(k.s_whi, 1)
            gn_statistics_act(act, gn, k)
            act.wait_ge(k.s_const, since(32))

            def norm_of(b):
                for ct in range(CT):
                    act.wait_ge(k.s_xn, since(CT * b + ct + 1))
                    act.activation(xh[:, ct, 0, :], xn[:, ct, :], ACT.Copy).then_inc(k.s_xhi, 1)

            def project(b):
                act.wait_ge(k.s_qout, since(32 * b))
                for i in range(2 * CT):
                    act.wait_ge(k.s_qk, since(2 * CT * b + i + 1))
                    act.wait_ge(k.s_qlo, since(earlier(b, i, 2, 2 * CT)))
                    act.activation(in_two(qf[:, i % 2, :]), halves(ps_s[:, i % 2]), ACT.Sigmoid,
                                   scale=kept.scale_of(NAMES[i // CT])).then_inc(k.s_sig, 1)
                    act.wait_ge(k.s_sig, since(2 * CT * b + i + 1))
                    act.activation(qh[:, i, 0, :], qf[:, i % 2, :], ACT.Copy, scale=Q_UP
                                   ).then_inc(k.s_qhi, 1)
                act.wait_ge(k.s_vlo, since(b))
                for t in range(NB):
                    act.wait_ge(k.s_vps, since(NB * b + t + 1))
                    act.activation(vf[:, t, :], ps_a[0:BP, t % 4, 0:C], ACT.Copy,
                                   scale=kept.scale_of("v", BP)).then_inc(k.s_vf, 1)

            def norm_v(b):
                act.wait_ge(k.s_n2, since(b + 1))
                act.activation(norm[:, 1, :], norm[:, 0, :], ACT.Sqrt).then_inc(k.s_n1, 1)
                act.wait_ge(k.s_vn, since(b + 1))
                act.wait_ge(k.s_av, since(HEADS * b))
                act.activation(v[:].rearrange("p t h d -> p (t h) d")[:, :, 0:HD],
                               vf[:].rearrange("p t (h d) -> p (t h) d", d=HD), ACT.Copy, scale=V_UP
                               ).then_inc(k.s_vhi, 1)

            def image(b, last):
                for n in range(NS):
                    if n == KEEP:
                        if not (isinstance(b, int) and b == 0):
                            act.wait_ge(k.s_yout, since(16 * b))
                        act.activation(xb[:, 1], xb[:, 0], ACT.Copy).then_inc(k.s_res, 1)
                    if n == AHEAD and not last:
                        norm_of(b + 1)
                    head, t = divmod(n, NB)
                    act.wait_ge(k.s_s, since(NS * b + n + 1))
                    act.wait_ge(k.s_sm, since((NW - 1) * earlier(b, n, SS, NS)))
                    act.wait_ge(k.s_smp, since(earlier(b, n, SS, NS)))
                    a, z = columns(0, t)
                    act.activation(sh[:, n % SS, 0, a:z], flat_s(n)[:, a:z], ACT.Copy,
                                   scale=S_DOWN).then_inc(k.s_shi, 1)
                    if t == 1 and head:
                        sums(act, b, head - 1)
                sums(act, b, HEADS - 1)
                if not last:
                    project(b + 1)
                for kt in range(KT):
                    for i, grp in enumerate(GROUPS):
                        n = 2 * kt + i
                        a, w = grp[0] * BP, len(grp) * BP
                        act.wait_ge(k.s_tr, since(2 * KT * b + n + 1))
                        act.activation(ot[:, kt, 0, a:a + w], ps_s[:, kt % 2, i, 0:w], ACT.Copy,
                                       scale=O_UP).then_inc(k.s_othi, 1)
                if not last:
                    norm_v(b + 1)
                for mt in range(CT):
                    act.wait_ge(k.s_ysum, since(2 * CT * b + 2 * mt + 2))
                    act.activation(xb[:, 1, mt, :], xb[:, 1, mt, :], ACT.Identity,
                                   bias=bo[:, mt:mt + 1]).then_inc(k.s_ybias, 1)

            norm_of(0)
            project(0)
            norm_v(0)
            with act.Fori(0, B - 1) as b:
                image(b, False)
            image(B - 1, True)

        @block.tensor
        def _(pe):
            gn_statistics_pe(pe, kept.grp, gn, k)
            pe.wait_ge(k.s_wlo, since(4))
            pe.wait_ge(k.s_ones, since(1))

            def scores(b, n):
                head, t = divmod(n, NB)
                pe.wait_ge(k.s_slo, since(earlier(b, n, 2, NS)))
                rs = columns(0, t)
                for h in range(2):
                    a, z = max(rs[0], 512 * h), min(rs[1], 512 * (h + 1))
                    mm = pe.matmul(flat_s(n)[:, a:z], stacks[:, 1, head, t * BP:(t + 1) * BP],
                                   stacks[:, 0, head, a:z], start=True, stop=True)
                mm.then_inc(k.s_s, 1)

            def project(b):
                pe.wait_ge(k.s_xlo, since(CT * (b + 1)))
                pe.wait_ge(k.s_slo, since(NS * b))
                for i in range(2 * CT):
                    pe.wait_ge(k.s_qhi, since(earlier(b, i, 2, 2 * CT)))
                    which, mt = divmod(i, CT)
                    for h in range(2):
                        for ct in range(CT):
                            mm = three_passes(
                                pe, ps_s[:, i % 2, h, 0:HALF],
                                lambda a: wqkv[:, a, ct, which, mt * 128:(mt + 1) * 128],
                                lambda a: xh[:, ct, a, h * HALF:(h + 1) * HALF], ct == 0,
                                ct == CT - 1)
                    mm.then_inc(k.s_qk, 1)
                pe.wait_ge(k.s_avs, since(BANKS * HEADS * b))
                for t in range(NB):
                    pe.wait_ge(k.s_vf, since(earlier(b, t, 4, NB)))
                    for ct in range(CT):
                        mm = three_passes(pe, ps_a[0:BP, t % 4, 0:C],
                                          lambda a: xh[:, ct, a, t * BP:(t + 1) * BP],
                                          lambda a: wqkv[:, a, ct, 2, :], ct == 0, ct == CT - 1)
                    mm.then_inc(k.s_vps, 1)

            def image(b, last):
                pe.wait_ge(k.s_stack, since(192 * (b + 1)))
                pe.wait_ge(k.s_vf, since(NB * (b + 1)))
                pe.wait_ge(k.s_otlo, since(2 * KT * b))
                pe.wait_ge(k.s_ysum, since(2 * CT * b))
                pe.wait_ge(k.s_vlo, since(b + 1))
                scores(b, 0)
                scores(b, 1)
                for n in range(NS):
                    head, t = divmod(n, NB)
                    if n + 2 < NS:
                        scores(b, n + 2)
                    if t == 0:
                        begun = set()
                    for w in (0, 2, 1):
                        if w == POOLS:
                            pe.wait_ge(k.s_smp, since(NS * b + n + 1))
                        else:
                            pe.wait_ge(k.s_sm, since((NW - 1) * (NS * b + n) + (1 if w == 0 else 2)))
                        rs = reached(w, t)
                        for r in rs:
                            if head and r // 2 not in begun:
                                pe.wait_ge(k.s_avs, since(BANKS * (HEADS * b + head - 1) + r // 2 + 1))
                            at = (r % 2) * CW + w * VW
                            for h, cols in ((0, VW), (1, HD + 1)):
                                mm = pe.matmul(ps_a[0:BP, r // 2, at:at + cols],
                                               sm[w][:, n % SS, h, (r - rs[0]) * BP:
                                                     (r - rs[0] + 1) * BP],
                                               v[:, t, head, 0:cols], start=r // 2 not in begun,
                                               stop=True, skip_group_check=True)
                                begun.add(r // 2)
                    mm.then_inc(k.s_avt if t < NB - 1 else k.s_av, 1)
                if not last:
                    project(b + 1)
                    pe.wait_ge(k.s_qhi, since(2 * CT * (b + 2)))
                for kt in range(KT):
                    pe.wait_ge(k.s_o, since(HEADS * (b + 1)))
                    pe.wait_ge(k.s_otlo, since(2 * KT * b + max(0, 2 * (kt - 1))))
                    for i, grp in enumerate(GROUPS):
                        for j, r in enumerate(grp):
                            w, ct = divmod(kt, CT)
                            mm = pe.transpose(ps_s[:, kt % 2, i, j * BP:(j + 1) * BP],
                                              o[0:BP, r * NW + w, ct * 128:(ct + 1) * 128],
                                              kept.ident[0:BP, 0:BP])
                        mm.then_inc(k.s_tr, 1)
                pe.wait_ge(k.s_otlo, since(2 * KT * (b + 1)))
                if not last:
                    pe.wait_ge(k.s_vf, since(NB * (b + 2)))
                pe.wait_ge(k.s_avs, since(BANKS * HEADS * (b + 1)))
                for mt in range(CT):
                    for i, grp in enumerate(GROUPS):
                        a, w = grp[0] * BP, len(grp) * BP
                        for kt in range(KT):
                            mm = three_passes(pe, ps_a[:, 2 * mt + i, 0:w],
                                              lambda a_: wo[:, a_, kt, mt * 128:(mt + 1) * 128],
                                              lambda a_: ot[:, kt, a_, a:a + w], kt == 0,
                                              kt == KT - 1)
                        mm.then_inc(k.s_y, 1)

            project(0)
            with pe.Fori(0, B - 1) as b:
                image(b, False)
            image(B - 1, True)




def build(nc, ins, out, upto=9, shown=()):
    def dram(name, shape, dt=F32):
        kind = {"kind": "ExternalOutput"} if name in shown else {}
        return nc.dram_tensor(name, shape, dt, **kind).ap()

    xT_d = dram("xT_d", [B, BP, NB * 2 * C], F16)
    pos1_d = dram("pos1_d", [B, NB, OFF * BP])
    pos2_d = dram("pos2_d", [B, NB, OFF * BP])
    h_d = dram("h_d", [B, NB, 128, HT * BP])
    x1_d = dram("x1_d", [B, 128, CT * PIX])
    q_d = dram("q_d", [2, CT, 128, 2, PIX], F16)
    def stage(number, run, *args):
        if number <= upto:
            before = nc.snapshot_sems()
            run(nc, kept, *args)
            nc.clear_and_free_semaphores(nc.allocated_since(before))
            nc.all_engine_barrier()

    with ExitStack() as ctx:
        kept = Kept(nc, ctx)
        with ExitStack() as c:
            wts = Weights(nc, c)
            stage(1, stage_norm, wts, ins["x"], ins["w1"], ins["woff1"], ins["boff1"], ins, xT_d,
                  pos1_d)
            stage(2, stage_layer1, wts, xT_d, pos1_d, h_d)
            stage(3, stage_offsets2, wts, ins["w2"], ins["woff2"], ins["boff2"], ins, h_d, pos2_d)
            stage(4, stage_layer2, wts, h_d, pos2_d, ins["x"], x1_d)
        stage(5, stage_attention, ins, x1_d, q_d, out)


def launch_arrays(x, w_p1, b_p1, w_m1, b_m1, w_c1, w_p2, b_p2, w_m2, b_m2, w_c2, Wq, Wk, Wv, Wout, bout):
    def offsets(w_p, w_m):
        w = np.concatenate([w_p, w_m], 0).reshape(OFF, -1, 128, TAPS)
        return np.ascontiguousarray(w.transpose(2, 1, 3, 0)).reshape(128, -1, OFF)

    first = w_c1.reshape(HID, CT, 128, TAPS).transpose(2, 1, 3, 0).reshape(128, -1)
    second = w_c2.reshape(C, HT, 128, TAPS).transpose(2, 3, 1, 0)
    pairs = second[:, :8].reshape(128, 4, 2, HT, C).transpose(0, 1, 3, 2, 4).reshape(128, -1)
    second = np.concatenate([pairs, second[:, 8].reshape(128, -1)], 1)
    qkv = np.stack([w.T for w in (Wq, Wk, Wv)], 0).reshape(3, CT, 128, C).transpose(2, 1, 0, 3)
    o = Wout.T.reshape(len(WINDOWS) * CT, 128, C).transpose(1, 0, 2)
    return {
        "x": x, "w1": first, "woff1": offsets(w_p1, w_m1),
        "boff1": np.concatenate([b_p1, b_m1])[:, None], "w2": second, "woff2": offsets(w_p2, w_m2),
        "boff2": np.concatenate([b_p2, b_m2])[:, None], "wqkv": qkv, "wout": o,
        "bout": bout.reshape(CT, 128).T,
    }


def kernel(**inputs):
    import concourse.bacc as bacc
    from concourse.bass_utils import run_bass_kernel_spmd

    given = {n.replace("L0_conv_", "").replace("L1_conv_", ""): np.asarray(a) for n, a in inputs.items()}
    arrays = launch_arrays(**given) | constants()
    arrays = {f"in_{n}": np.ascontiguousarray(a) for n, a in arrays.items()}
    nc = bacc.Bacc("TRN2", target_bir_lowering=False, num_devices=1)
    ins = {n[3:]: nc.dram_tensor(n, a.shape, mybir.dt.from_np(a.dtype), kind="ExternalInput").ap()
           for n, a in arrays.items()}
    out = nc.dram_tensor("out", (B, C, S, S), F32, kind="ExternalOutput").ap()
    build(nc, ins, out)
    got = run_bass_kernel_spmd(nc, [arrays], core_ids=[0])
    return got.results[0]["out"]
```
